# Optimizing a Trainium2 kernel written in Bass

```python
import numpy as np
import jax
import jax.numpy as jnp

def _softmax(x, axis=-1):
    return jax.nn.softmax(x, axis=axis)

def _gelu(x):
    return jax.nn.gelu(x, approximate=True)

def _silu(x):
    return jax.nn.silu(x)

def _sigmoid(x):
    return jax.nn.sigmoid(x)

def _layernorm(x, axis=-1, eps=1e-05):
    m = jnp.mean(x, axis=axis, keepdims=True)
    v = jnp.var(x, axis=axis, keepdims=True)
    return (x - m) / jnp.sqrt(v + eps)

def _scatter_add(tgt, idx, src, axis=0):
    return tgt.at[idx].add(src)

def _segment_sum(src, seg, n):
    return jax.ops.segment_sum(src, seg, n)
kernel_name = 'mk_gnn_ffn_d1_gnn_r8_df4d04'

def setup_inputs(seed: int=0):
    np.random.seed(seed)
    _w = jnp.asarray

    def _rec_inputs():
        import jax
        import jax.numpy as jnp
        _gk = jax.random.key(seed)
        x = -0.0003713 + 1 * jax.random.normal(jax.random.fold_in(_gk, 1), (12500, 256), jnp.float32)
        src = jax.random.randint(jax.random.fold_in(_gk, 2), (200000,), 0, 12500, jnp.int32)
        dst = jax.random.randint(jax.random.fold_in(_gk, 3), (200000,), 0, 12500, jnp.int32)
        _o = jnp.argsort(dst, stable=True)
        src = src[_o]
        dst = dst[_o]
        return (x, src, dst)
    x, src, dst = _rec_inputs()

    def _L0_gnn_setup():
        import jax, jax.numpy as jnp
        import numpy as np
        N, E = (6250, 100000)
        IN_C, HID_C, OUT_C = (256, 256, 256)

        def _gcn_prep(edge_index, n_nodes):
            src = jnp.concatenate([edge_index[0], jnp.arange(n_nodes, dtype=edge_index.dtype)])
            dst = jnp.concatenate([edge_index[1], jnp.arange(n_nodes, dtype=edge_index.dtype)])
            deg = jax.ops.segment_sum(jnp.ones_like(dst, dtype=jnp.float32), dst, num_segments=n_nodes)
            deg_inv_sqrt = jnp.where(deg > 0, jax.lax.rsqrt(jnp.maximum(deg, 1.0)), 0.0)
            norm = deg_inv_sqrt[src] * deg_inv_sqrt[dst]
            return (src, dst, norm)

        def _gcn_layer(x, src, dst, norm, W, b, n_nodes):
            h = x @ W
            msg = h[src] * norm[:, None]
            out = jax.ops.segment_sum(msg, dst, num_segments=n_nodes)
            return out + b
        key = jax.random.key(seed)
        ks = jax.random.split(key, 8)
        x_piece = jax.random.normal(ks[0], (N, IN_C), dtype=jnp.float32)
        edge_index_piece = jax.random.randint(ks[1], (2, E), 0, N, dtype=jnp.int64)
        batch = jnp.zeros((N,), dtype=jnp.int64)

        def glorot(k, fan_in, fan_out):
            s = jnp.sqrt(6.0 / (fan_in + fan_out)).astype(jnp.float32)
            return jax.random.uniform(k, (fan_in, fan_out), jnp.float32, -s, s)
        return {'x_piece': x_piece, 'edge_index_piece': edge_index_piece, 'batch': batch, 'W1': glorot(ks[2], IN_C, HID_C), 'b1': jnp.zeros((HID_C,), jnp.float32), 'W2': glorot(ks[3], HID_C, HID_C), 'b2': jnp.zeros((HID_C,), jnp.float32), 'W3': glorot(ks[4], HID_C, OUT_C), 'b3': jnp.zeros((OUT_C,), jnp.float32)}
    _L0_gnn_all = _L0_gnn_setup()
    _L0_gnn_in = {k: v for k, v in _L0_gnn_all.items() if k in ('W1', 'b1', 'W2', 'b2', 'W3', 'b3')}
    del _L0_gnn_all

    def _L0_ffn_setup():
        import jax, jax.numpy as jnp
        import numpy as np
        B, N, D = (16, 512, 256)
        NUM_EXPERTS, TOP_K, HEADS = (4, 2, 4)
        N_EDGES = 131072
        LN_EPS = 1e-05

        def _layernorm(x, g, b):
            mu = x.mean(-1, keepdims=True)
            var = ((x - mu) ** 2).mean(-1, keepdims=True)
            return (x - mu) * jax.lax.rsqrt(var + LN_EPS) * g + b

        def _forward(x, edge_index, W_gat, att_src, att_dst, b_gat, ln_gamma, ln_beta, W1, b1, W2, b2):
            Bc, Nc, Dc = x.shape
            M = Bc * Nc
            x_flat = x.reshape(M, Dc)
            h = (x_flat @ W_gat).reshape(M, HEADS, NUM_EXPERTS)
            loops = jnp.arange(M, dtype=edge_index.dtype)
            src = jnp.concatenate([edge_index[0], loops])
            dst = jnp.concatenate([edge_index[1], loops])
            a_src = (h * att_src).sum(-1)
            a_dst = (h * att_dst).sum(-1)
            e = jax.nn.leaky_relu(a_src[src] + a_dst[dst], negative_slope=0.2)
            e_max = jax.ops.segment_max(e, dst, num_segments=M)
            ee = jnp.exp(e - e_max[dst])
            denom = jax.ops.segment_sum(ee, dst, num_segments=M)
            alpha = ee / (denom[dst] + 1e-16)
            msg = h[src] * alpha[:, :, None]
            agg = jax.ops.segment_sum(msg, dst, num_segments=M).reshape(M, HEADS * NUM_EXPERTS) + b_gat
            scores = _layernorm(agg, ln_gamma, ln_beta).reshape(M, HEADS, NUM_EXPERTS).mean(1)
            scores = scores.reshape(Bc, Nc, NUM_EXPERTS)
            topk_s, topk_i = jax.lax.top_k(scores, TOP_K)
            w = jax.nn.softmax(topk_s, axis=-1)
            out = jnp.zeros_like(x)
            for ei in range(NUM_EXPERTS):
                g = jnp.where(topk_i == ei, w, 0.0).sum(-1)
                hh = jax.nn.gelu(x @ W1[ei] + b1[ei], approximate=False)
                out = out + g[..., None] * (hh @ W2[ei] + b2[ei])
            return out
        key = jax.random.key(seed)
        ks = jax.random.split(key, 8)
        s = 0.05
        return {'x': jax.random.normal(ks[0], (B, N, D), jnp.float32), 'W_gat': jax.random.normal(ks[1], (D, HEADS * NUM_EXPERTS), jnp.float32) * s, 'att_src': jax.random.normal(ks[2], (HEADS, NUM_EXPERTS), jnp.float32) * s, 'att_dst': jax.random.normal(ks[3], (HEADS, NUM_EXPERTS), jnp.float32) * s, 'b_gat': jnp.zeros((HEADS * NUM_EXPERTS,), jnp.float32), 'ln_gamma': jnp.ones((HEADS * NUM_EXPERTS,), jnp.float32), 'ln_beta': jnp.zeros((HEADS * NUM_EXPERTS,), jnp.float32), 'W1': jax.random.normal(ks[4], (NUM_EXPERTS, D, 2 * D), jnp.float32) * s, 'b1': jnp.zeros((NUM_EXPERTS, 2 * D), jnp.float32), 'W2': jax.random.normal(ks[5], (NUM_EXPERTS, 2 * D, D), jnp.float32) * s, 'b2': jnp.zeros((NUM_EXPERTS, D), jnp.float32), 'edge_index': jax.random.randint(ks[6], (2, N_EDGES), 0, B * N, jnp.int32)}
    _L0_ffn_all = _L0_ffn_setup()
    _L0_ffn_in = {k: v for k, v in _L0_ffn_all.items() if k in ('W_gat', 'att_src', 'att_dst', 'b_gat', 'ln_gamma', 'ln_beta', 'W1', 'b1', 'W2', 'b2', 'edge_index')}
    del _L0_ffn_all
    return {'x': x, 'src': src, 'dst': dst, 'L0_gnn_W1': _L0_gnn_in['W1'], 'L0_gnn_b1': _L0_gnn_in['b1'], 'L0_gnn_W2': _L0_gnn_in['W2'], 'L0_gnn_b2': _L0_gnn_in['b2'], 'L0_gnn_W3': _L0_gnn_in['W3'], 'L0_gnn_b3': _L0_gnn_in['b3'], 'L0_ffn_W_gat': _L0_ffn_in['W_gat'], 'L0_ffn_att_src': _L0_ffn_in['att_src'], 'L0_ffn_att_dst': _L0_ffn_in['att_dst'], 'L0_ffn_b_gat': _L0_ffn_in['b_gat'], 'L0_ffn_ln_gamma': _L0_ffn_in['ln_gamma'], 'L0_ffn_ln_beta': _L0_ffn_in['ln_beta'], 'L0_ffn_W1': _L0_ffn_in['W1'], 'L0_ffn_b1': _L0_ffn_in['b1'], 'L0_ffn_W2': _L0_ffn_in['W2'], 'L0_ffn_b2': _L0_ffn_in['b2'], 'L0_ffn_edge_index': _L0_ffn_in['edge_index']}

def reference(x, src, dst, L0_gnn_W1, L0_gnn_b1, L0_gnn_W2, L0_gnn_b2, L0_gnn_W3, L0_gnn_b3, L0_ffn_W_gat, L0_ffn_att_src, L0_ffn_att_dst, L0_ffn_b_gat, L0_ffn_ln_gamma, L0_ffn_ln_beta, L0_ffn_W1, L0_ffn_b1, L0_ffn_W2, L0_ffn_b2, L0_ffn_edge_index):
    import jax
    import jax.numpy as jnp

    def _L0_gnn_ref(x_piece, edge_index_piece, batch, W1, b1, W2, b2, W3, b3):
        import jax, jax.numpy as jnp
        import numpy as np
        N, E = (6250, 100000)
        IN_C, HID_C, OUT_C = (256, 256, 256)

        def _gcn_prep(edge_index, n_nodes):
            src = jnp.concatenate([edge_index[0], jnp.arange(n_nodes, dtype=edge_index.dtype)])
            dst = jnp.concatenate([edge_index[1], jnp.arange(n_nodes, dtype=edge_index.dtype)])
            deg = jax.ops.segment_sum(jnp.ones_like(dst, dtype=jnp.float32), dst, num_segments=n_nodes)
            deg_inv_sqrt = jnp.where(deg > 0, jax.lax.rsqrt(jnp.maximum(deg, 1.0)), 0.0)
            norm = deg_inv_sqrt[src] * deg_inv_sqrt[dst]
            return (src, dst, norm)

        def _gcn_layer(x, src, dst, norm, W, b, n_nodes):
            h = x @ W
            msg = h[src] * norm[:, None]
            out = jax.ops.segment_sum(msg, dst, num_segments=n_nodes)
            return out + b
        n_nodes = x_piece.shape[0]
        src, dst, norm = _gcn_prep(edge_index_piece, n_nodes)
        x = _gcn_layer(x_piece, src, dst, norm, W1, b1, n_nodes)
        x = jax.nn.gelu(x)
        x = _gcn_layer(x, src, dst, norm, W2, b2, n_nodes)
        x = jax.nn.gelu(x)
        x = _gcn_layer(x, src, dst, norm, W3, b3, n_nodes)
        return x

    def _L0_ffn_ref(x, W_gat, att_src, att_dst, b_gat, ln_gamma, ln_beta, W1, b1, W2, b2, edge_index):
        import jax, jax.numpy as jnp
        import numpy as np
        B, N, D = (16, 512, 256)
        NUM_EXPERTS, TOP_K, HEADS = (4, 2, 4)
        N_EDGES = 131072
        LN_EPS = 1e-05

        def _layernorm(x, g, b):
            mu = x.mean(-1, keepdims=True)
            var = ((x - mu) ** 2).mean(-1, keepdims=True)
            return (x - mu) * jax.lax.rsqrt(var + LN_EPS) * g + b

        def _forward(x, edge_index, W_gat, att_src, att_dst, b_gat, ln_gamma, ln_beta, W1, b1, W2, b2):
            Bc, Nc, Dc = x.shape
            M = Bc * Nc
            x_flat = x.reshape(M, Dc)
            h = (x_flat @ W_gat).reshape(M, HEADS, NUM_EXPERTS)
            loops = jnp.arange(M, dtype=edge_index.dtype)
            src = jnp.concatenate([edge_index[0], loops])
            dst = jnp.concatenate([edge_index[1], loops])
            a_src = (h * att_src).sum(-1)
            a_dst = (h * att_dst).sum(-1)
            e = jax.nn.leaky_relu(a_src[src] + a_dst[dst], negative_slope=0.2)
            e_max = jax.ops.segment_max(e, dst, num_segments=M)
            ee = jnp.exp(e - e_max[dst])
            denom = jax.ops.segment_sum(ee, dst, num_segments=M)
            alpha = ee / (denom[dst] + 1e-16)
            msg = h[src] * alpha[:, :, None]
            agg = jax.ops.segment_sum(msg, dst, num_segments=M).reshape(M, HEADS * NUM_EXPERTS) + b_gat
            scores = _layernorm(agg, ln_gamma, ln_beta).reshape(M, HEADS, NUM_EXPERTS).mean(1)
            scores = scores.reshape(Bc, Nc, NUM_EXPERTS)
            topk_s, topk_i = jax.lax.top_k(scores, TOP_K)
            w = jax.nn.softmax(topk_s, axis=-1)
            out = jnp.zeros_like(x)
            for ei in range(NUM_EXPERTS):
                g = jnp.where(topk_i == ei, w, 0.0).sum(-1)
                hh = jax.nn.gelu(x @ W1[ei] + b1[ei], approximate=False)
                out = out + g[..., None] * (hh @ W2[ei] + b2[ei])
            return out
        return _forward(x, edge_index, W_gat, att_src, att_dst, b_gat, ln_gamma, ln_beta, W1, b1, W2, b2)
    edge_index = jnp.stack([src, dst])
    batch0 = jnp.zeros((12500,), jnp.int32)
    x = x + _L0_gnn_ref(_layernorm(x, axis=-1), edge_index, batch0, L0_gnn_W1, L0_gnn_b1, L0_gnn_W2, L0_gnn_b2, L0_gnn_W3, L0_gnn_b3)
    x = x + _L0_ffn_ref(_layernorm(x, axis=-1)[None], L0_ffn_W_gat, L0_ffn_att_src, L0_ffn_att_dst, L0_ffn_b_gat, L0_ffn_ln_gamma, L0_ffn_ln_beta, L0_ffn_W1, L0_ffn_b1, L0_ffn_W2, L0_ffn_b2, L0_ffn_edge_index)[0]
    return x

_drawn_inputs = setup_inputs


def setup_inputs(seed=0):
    import zlib

    import numpy as np

    out = dict(_drawn_inputs(seed))
    spreads = {'L0_gnn_b1': (0.0, 0.1),
     'L0_gnn_b2': (0.0, 0.1),
     'L0_gnn_b3': (0.0, 0.1),
     'L0_ffn_b_gat': (0.0, 0.1),
     'L0_ffn_ln_gamma': (1.0, 0.2),
     'L0_ffn_ln_beta': (0.0, 0.1),
     'L0_ffn_b1': (0.0, 0.1),
     'L0_ffn_b2': (0.0, 0.1)}
    factors = {}
    for name, (base, spread) in spreads.items():
        noise = np.random.default_rng([zlib.crc32(name.encode()), seed]).standard_normal(out[name].shape)
        drawn = base * np.exp(spread * noise) if base else spread * noise
        out[name] = jnp.asarray(drawn.astype(out[name].dtype))
    for name, factor in factors.items():
        out[name] = (out[name] * factor).astype(out[name].dtype)
    return out
```

```python
from contextlib import ExitStack

import concourse.bass as bass
from concourse import mybir

ALU = mybir.AluOpType
ACT = mybir.ActivationFunctionType
F32 = mybir.dt.float32
BF16 = mybir.dt.bfloat16
I32 = mybir.dt.int32
AX = mybir.AxisListType

P = 128
U = 16
SRC_BITS = 14
NO_DST = 255
BIG = -3.0e38
EPS = 1e-5


def steps_for(edges, blocks):
    unit = P
    need = -(-edges // P) + blocks - 1
    return -(-need // unit) * unit


class Chain:

    def __init__(self, eng, sem):
        self.eng, self.sem, self.n = eng, sem, 0

    def __call__(self, ins):
        ins.then_inc(self.sem, 1)
        self.n += 1
        self.eng.wait_ge(self.sem, self.n)


def build(nc, x, src, dst, gnn_w, gnn_b, w_gat, att_src, att_dst, b_gat, ln_gamma, ln_beta,
          ew1, eb1, ew2, eb2, edges2, out):
    N, D = x.shape
    NB = -(-N // P)
    TAIL = N - (NB - 1) * P
    KD = D // P
    NE, _, HID = ew1.shape
    KH = HID // P
    HE = w_gat.shape[1]
    NH = HE // NE
    GW = HE + NH
    E1, E2 = src.shape[0], edges2.shape[1]
    S1, S2 = steps_for(E1, NB), steps_for(E2, NB)
    PAIRS = NB // 2
    assert NB % 2 == 0 and N < 1 << SRC_BITS

    table = nc.dram_tensor("feature_table", (NB * P, D), F32).ap()
    gat_table = nc.dram_tensor("attention_table", (NB * P, GW), F32).ap()
    x1_dram = nc.dram_tensor("x_after_gnn", (NB * P, D), F32).ap()
    xnt_dram = nc.dram_tensor("x_normed_t", (NB, P, KD * P), F32).ap()
    list_dram = [nc.dram_tensor(f"edge_list{i}", (P * s, 1), I32).ap() for i, s in enumerate((S1, S2))]
    blk_dram = [nc.dram_tensor(f"step_block{i}", (s,), I32).ap() for i, s in enumerate((S1, S2))]

    with ExitStack() as ctx:
        def sb(name, shape, dt=F32):
            return ctx.enter_context(nc.sbuf_tensor(name, shape, dt))

        phase_sems = []

        def sem(name):
            s = nc.alloc_semaphore(name=name)
            phase_sems.append(s)
            return s

        def end_phase():
            with nc.Block() as block:
                @block.gpsimd
                def _(pool):
                    for s in phase_sems:
                        pool.sem_clear(s)
            for s in phase_sems:
                nc.release_semaphore(s)
            phase_sems.clear()

        ps = ctx.enter_context(nc.psum_tensor("ps", [P, 8, 512], F32))
        acc = sb("acc", [P, NB * D])
        iota = sb("iota", [P, P])
        ident = sb("ident", [P, P])
        ident_bf = sb("ident_bf", [P, P], BF16)
        lower = sb("lower", [P, P])
        ones = sb("ones", [P, P])
        zeros = sb("zeros", [P, P])
        step_no = sb("step_no", [P, S1 // P])
        idx = [sb("idx1", [P, S1], I32), sb("idx2", [P, S2], I32)]
        dloc = [sb("dloc1", [P, S1]), sb("dloc2", [P, S2])]
        blk = [sb("blk1", [1, S1], I32), sb("blk2", [1, S2], I32)]
        dinv = sb("dinv", [P, NB])
        onehot = sb("onehot", [P, 2, U, P])
        work = sb("work", [P, 2 * U * D])
        stage = sb("stage", [P, 2, U], I32)
        rec_stage = sb("rec_stage", [P, 2, U], I32)
        stats = sb("stats", [P, NB, 6])
        mv = sb("mv", [P, NB, 2])
        rstd = sb("rstd", [P, NB])
        eps = sb("eps", [P, 1])
        gw_sb = sb("gw_sb", [P, 3, KD, D])
        gb_sb = sb("gb_sb", [1, 3, D])
        HG = sb("HG", [P, NB, GW])
        ad = sb("ad", [P, NB, NH])
        emx = sb("emx", [P, NB, NH])
        V = work[:, 4800:4800 + NB * 2 * NH].rearrange("p (b f) -> p b f", f=2 * NH)
        AGG = acc[:, S2 * GW:(S2 + NB) * GW].rearrange("p (b f) -> p b f", f=GW)
        small = work[:, 2 * U * D - 3 * NB * HE:].rearrange("p (a b e) -> p a b e", a=3, b=NB)
        row16 = sb("row16", [P, 5, HE])
        wg_sb = sb("wg_sb", [P, KD, HE])
        gates = sb("gates", [P, NB, NE])

        s_held = ctx.enter_context(nc.semaphore("held"))

        def hold(eng, s, value):
            eng.wait_ge(s, value)
            eng.sem_inc(s_held, 1)

        s_c, s_iota = sem("constants_ready"), sem("iota_done")
        s_cd = sem("constant_chain")
        s_w = sem("weights_loaded")
        with nc.Block() as block:
            @block.gpsimd
            def _(pool):
                nc.gpsimd.iota(iota[:], pattern=[[1, P]], base=0, channel_multiplier=0,
                               allow_small_or_imprecise_dtypes=True)
                nc.gpsimd.iota(step_no[:], pattern=[[P, S1 // P]], base=0, channel_multiplier=1,
                               allow_small_or_imprecise_dtypes=True)
                nc.gpsimd.memset(ident[:], 0.0)
                nc.gpsimd.memset(ones[:], 1.0)
                nc.gpsimd.memset(zeros[:], 0.0)
                nc.gpsimd.memset(eps[:], EPS)
                nc.gpsimd.memset(lower[:], 1.0).then_inc(s_iota, 1)
                pool.wait_ge(s_iota, 1)
                nc.gpsimd.affine_select(out=ident[:], in_=ident[:], compare_op=ALU.not_equal, fill=1.0,
                                        base=0, pattern=[[-1, P]], channel_multiplier=1)
                nc.gpsimd.affine_select(out=lower[:], in_=lower[:], compare_op=ALU.is_gt, fill=0.0,
                                        base=0, pattern=[[1, P]], channel_multiplier=-1).then_inc(s_c, 1)

            @block.vector
            def _(dve):
                dve.wait_ge(s_c, 1)
                nc.vector.tensor_copy(ident_bf[:], ident[:]).then_inc(s_cd, 1)

            @block.sync
            def _(sp):
                for i in range(3):
                    sp.dma_start(gw_sb[:, i], gnn_w[i].rearrange("(k p) n -> p k n", p=P)).then_inc(s_w, 16)
                    sp.dma_start(gb_sb[0:1, i], gnn_b[i].rearrange("(a n) -> a n", a=1)).then_inc(s_w, 16)
                sp.dma_start(wg_sb[:], w_gat.rearrange("(k p) n -> p k n", p=P)).then_inc(s_w, 16)
                for i, v in enumerate((att_src.rearrange("h e -> (h e)"), att_dst.rearrange("h e -> (h e)"),
                                       b_gat, ln_gamma, ln_beta)):
                    sp.dma_start(row16[:, i], v.rearrange("(a n) -> a n", a=1).broadcast_to([P, HE])).then_inc(s_w, 16)
                sp.wait_ge(s_w, 16 * 12)

        end_phase()

        def group(i, src_ap, dst_ap, rows, cols, S, want_degree):
            at = [0]

            def area(n, dt=F32):
                a = acc[:, at[0]:at[0] + n]
                at[0] += n
                return a.bitcast(dt) if dt != F32 else a
            dst_i, src_i, blk_i = area(cols, I32), area(cols, I32), area(cols, I32)
            blk_f, dl_f, hot, cum, pos = (area(cols) for _ in range(5))
            listed, pads = area(S, I32), area(S, I32)
            assert at[0] <= NB * D
            cnt = small[:, 0].rearrange("p b e -> p (b e)")[:, 0:NB]
            tot = small[:, 0].rearrange("p b e -> p (b e)")[:, NB:2 * NB]
            incl = small[:, 0].rearrange("p b e -> p (b e)")[:, 2 * NB:3 * NB]
            first = small[:, 0].rearrange("p b e -> p (b e)")[:, 3 * NB:4 * NB]
            base = small[:, 0].rearrange("p b e -> p (b e)")[:, 4 * NB:5 * NB]
            q = small[:, 0].rearrange("p b e -> p (b e)")[:, 5 * NB:6 * NB]
            q_i = small[:, 0].rearrange("p b e -> p (b e)")[:, 6 * NB:7 * NB].bitcast(I32)
            hits = small[:, 0].rearrange("p b e -> p (b e)")[:, 7 * NB:8 * NB]
            bs = small[:, 1].rearrange("p b e -> p (b e)")[:, 0:S // P]
            bs_i = small[:, 1].rearrange("p b e -> p (b e)")[:, 64:64 + S // P].bitcast(I32)
            n = f"_{i}"
            s_in, s_cnt, s_pre, s_flat = sem("edges_in" + n), sem("counted" + n), sem("prefix_done" + n), sem("places_done" + n)
            s_padm, s_pad = sem("pads_made" + n), sem("pads_stored" + n)
            s_stg = sem("scatter_staged" + n)
            s_half = [sem(f"scattered{h}" + n) for h in range(2)]
            s_tick = sem("pool_tick" + n)
            s_list, s_bs, s_bsd, s_bsl = sem("list_in" + n), sem("step_blocks" + n), sem("step_blocks_out" + n), sem("step_blocks_in" + n)
            s_d = sem("dve_chain" + n)
            s_hot, s_hotfree, s_deg, s_sq = sem("degree_hots" + n), sem("degree_hots_used" + n), sem("degree_done" + n), sem("sqrt_done" + n)
            flat = dst_i
            HALVES = cols // U
            assert cols % (2 * U) == 0
            hot_bf = onehot[:].rearrange("p a u m -> p (a u m)").bitcast(BF16).rearrange(
                "p (a u m) -> p a u m", a=4, u=U)
            dl_hot = [hot_bf[0:rows, a] for a in range(2)]
            b_hot = [hot_bf[0:rows, 2 + a, :, 0:NB] for a in range(2)]

            with nc.Block() as block:
                @block.sync
                def _(sp):
                    sp.dma_start(dst_i[0:rows], dst_ap).then_inc(s_in, 16)
                    sp.dma_start(src_i[0:rows], src_ap).then_inc(s_in, 16)
                    sp.wait_ge(s_padm, 1)
                    sp.dma_start(list_dram[i].rearrange("(p s) a -> p (s a)", p=P), pads).then_inc(s_pad, 16)
                    sp.wait_ge(s_bs, 1)
                    sp.dma_start(blk_dram[i].rearrange("(j p) -> p j", p=P), bs_i, allow_slow_non_contiguous=True).then_inc(s_bsd, 16)
                    sp.wait_ge(s_bsd, 16)
                    sp.dma_start(blk[i][:], blk_dram[i].rearrange("(a s) -> a s", a=1)).then_inc(s_bsl, 16)
                    sp.wait_ge(s_bsl, 16)
                    for h in range(2):
                        sp.wait_ge(s_half[h], 16 * U * (HALVES // 2))
                    sp.dma_start(listed, list_dram[i].rearrange("(p s) a -> p (s a)", p=P)).then_inc(s_list, 16)

                @block.vector
                def _(dve):
                    link = Chain(dve, s_d)
                    dve.memset(pads, NO_DST << SRC_BITS).then_inc(s_padm, 1)
                    dve.wait_ge(s_in, 32)
                    nc.vector.tensor_scalar(blk_i[0:rows], dst_i[0:rows], 7, None, ALU.logical_shift_right)
                    link(nc.vector.tensor_scalar(dst_i[0:rows], dst_i[0:rows], P - 1, None, ALU.bitwise_and))
                    nc.vector.tensor_copy(blk_f[0:rows], blk_i[0:rows])
                    nc.vector.tensor_copy(dl_f[0:rows], dst_i[0:rows])
                    link(nc.vector.tensor_scalar(dst_i[0:rows], dst_i[0:rows], SRC_BITS, None, ALU.logical_shift_left))
                    link(nc.vector.tensor_tensor(src_i[0:rows], src_i[0:rows], dst_i[0:rows], ALU.bitwise_or))
                    with dve.Fori(0, NB) as b:
                        nc.vector.tensor_scalar(hot[0:rows], blk_f[0:rows], iota[0:rows, bass.ds(b, 1)], 0.0,
                                                ALU.is_equal, ALU.add,
                                                accum_out=cnt[0:rows, bass.ds(b, 1)]).then_inc(s_cnt, 1)
                        dve.wait_ge(s_cnt, b + 1)
                    dve.wait_ge(s_pre, 1)
                    link(nc.vector.tensor_copy(tot, ps[:, 0, 0:NB]))
                    link(nc.vector.tensor_tensor_scan(incl, tot, tot, 0.0, ALU.add, ALU.max))
                    link(nc.vector.tensor_tensor(first, incl, tot, ALU.subtract))
                    link(nc.vector.scalar_tensor_tensor(base, ps[:, 0, NB:2 * NB], -1.0, first, ALU.add, ALU.add))
                    link(nc.vector.tensor_copy(q_i, first))
                    link(nc.vector.tensor_scalar(q_i, q_i, 7, None, ALU.logical_shift_right))
                    link(nc.vector.tensor_copy(q, q_i))
                    link(nc.vector.tensor_tensor(q, q, iota[:, 0:NB], ALU.add))
                    for j in range(S // P):
                        link(nc.vector.tensor_scalar(hits, q, step_no[:, j:j + 1], 0.0, ALU.is_le, ALU.add,
                                                     accum_out=bs[:, j:j + 1]))
                    link(nc.vector.tensor_scalar(bs, bs, -1.0, None, ALU.add))
                    nc.vector.tensor_copy(bs_i, bs).then_inc(s_bs, 1)
                    link(nc.vector.memset(pos[0:rows], 0.0))
                    k0 = link.n
                    with dve.Fori(0, NB) as b:
                        nc.vector.tensor_scalar(hot[0:rows], blk_f[0:rows], iota[0:rows, bass.ds(b, 1)], None,
                                                ALU.is_equal).then_inc(s_d, 1)
                        dve.wait_ge(s_d, b * 4 + (k0 + 1))
                        nc.vector.tensor_tensor_scan(cum[0:rows], hot[0:rows], hot[0:rows], 0.0,
                                                     ALU.add, ALU.max).then_inc(s_d, 1)
                        dve.wait_ge(s_d, b * 4 + (k0 + 2))
                        nc.vector.scalar_tensor_tensor(cum[0:rows], cum[0:rows], base[0:rows, bass.ds(b, 1)],
                                                       hot[0:rows], ALU.add, ALU.mult).then_inc(s_d, 1)
                        dve.wait_ge(s_d, b * 4 + (k0 + 3))
                        nc.vector.tensor_tensor(pos[0:rows], pos[0:rows], cum[0:rows], ALU.add).then_inc(s_d, 1)
                        dve.wait_ge(s_d, b * 4 + (k0 + 4))
                    link.n += 4 * NB
                    link(nc.vector.tensor_copy(dst_i[0:rows], pos[0:rows]))
                    link(nc.vector.tensor_scalar(blk_i[0:rows], dst_i[0:rows], 7, None, ALU.logical_shift_right))
                    link(nc.vector.tensor_scalar(dst_i[0:rows], dst_i[0:rows], P - 1, None, ALU.bitwise_and))
                    nc.vector.tensor_copy(cum[0:rows], blk_i[0:rows])
                    link(nc.vector.tensor_copy(pos[0:rows], dst_i[0:rows]))
                    link(nc.vector.tensor_tensor(cum[0:rows], cum[0:rows], blk_f[0:rows], ALU.add))
                    link(nc.vector.scalar_tensor_tensor(pos[0:rows], pos[0:rows], float(S), cum[0:rows],
                                                        ALU.mult, ALU.add))
                    nc.vector.tensor_copy(flat[0:rows], pos[0:rows]).then_inc(s_flat, 1)
                    if want_degree:
                        dve.sem_inc(s_hotfree, 2)
                        with dve.Fori(0, HALVES // 2) as g:
                            for a in range(2):
                                dve.wait_ge(s_hotfree, g * 2 + (a + 1))
                                at_c = g * (2 * U) + a * U
                                nc.vector.tensor_tensor(
                                    dl_hot[a], iota[0:rows].unsqueeze(1).broadcast_to([rows, U, P]),
                                    dl_f[0:rows, bass.ds(at_c, U)].unsqueeze(2).broadcast_to([rows, U, P]),
                                    ALU.is_equal)
                                nc.vector.tensor_tensor(
                                    b_hot[a], iota[0:rows, 0:NB].unsqueeze(1).broadcast_to([rows, U, NB]),
                                    blk_f[0:rows, bass.ds(at_c, U)].unsqueeze(2).broadcast_to([rows, U, NB]),
                                    ALU.is_equal).then_inc(s_hot, 1)
                        dve.wait_ge(s_sq, 1)
                        nc.vector.reciprocal(dinv[:], dinv[:]).then_inc(s_d, 1)
                        link.n += 1
                    dve.wait_ge(s_list, 16)
                    nc.vector.tensor_scalar(idx[i][:], listed, (1 << SRC_BITS) - 1, None, ALU.bitwise_and)
                    link(nc.vector.tensor_scalar(pads, listed, SRC_BITS, None, ALU.logical_shift_right))
                    link(nc.vector.tensor_copy(dloc[i][:], pads))

                @block.tensor
                def _(pe):
                    pe.wait_ge(s_cnt, NB)
                    nc.tensor.matmul(ps[:, 0, 0:NB], ones[0:rows], cnt[0:rows], start=True, stop=True)
                    nc.tensor.matmul(ps[:, 0, NB:2 * NB], lower[0:rows], cnt[0:rows], start=True,
                                     stop=True).then_inc(s_pre, 1)
                    if want_degree:
                        nc.tensor.matmul(ps[:, 1, 0:NB], ident[:], ones[:, 0:NB], start=True, stop=False)
                        with pe.Fori(0, HALVES // 2) as g:
                            for a in range(2):
                                pe.wait_ge(s_hot, g * 2 + (a + 1))
                                for k in range(U):
                                    mm = nc.tensor.matmul(ps[:, 1, 0:NB], dl_hot[a][:, k], b_hot[a][:, k],
                                                          start=False, stop=False)
                                mm.then_inc(s_hotfree, 1)
                        nc.tensor.matmul(ps[:, 1, 0:NB], ident[:], zeros[:, 0:NB], start=False,
                                         stop=True).then_inc(s_deg, 1)

                @block.scalar
                def _(act):
                    if want_degree:
                        act.wait_ge(s_deg, 1)
                        nc.scalar.activation(dinv[:], ps[:, 1, 0:NB], ACT.Sqrt).then_inc(s_sq, 1)

                @block.gpsimd
                def _(pool):
                    pool.wait_ge(s_flat, 1)
                    pool.wait_ge(s_pad, 16)
                    for h in range(2):
                        pool.sem_inc(s_half[h], 0) if False else None
                    def half(g, h):
                        nc.gpsimd.tensor_copy(stage[0:rows, h], flat[0:rows, bass.ds(g * (2 * U) + h * U, U)])
                        nc.gpsimd.tensor_copy(rec_stage[0:rows, h],
                                              src_i[0:rows, bass.ds(g * (2 * U) + h * U, U)]).then_inc(s_stg, 1)

                    def scatter(h):
                        for k in range(U):
                            nc.gpsimd.indirect_dma_start(
                                out=list_dram[i], out_offset=bass.IndirectOffsetOnAxis(ap=stage[0:rows, h, k:k + 1], axis=0),
                                in_=rec_stage[0:rows, h, k:k + 1], in_offset=None).then_inc(s_half[h], 16)
                    for h in range(2):
                        half(0, h)
                        pool.wait_ge(s_stg, h + 1)
                        scatter(h)
                    with pool.Fori(1, HALVES // 2) as g:
                        for h in range(2):
                            pool.wait_ge(s_half[h], g * (16 * U))
                            pool.sem_inc(s_tick, 1)
                            half(g, h)
                            pool.wait_ge(s_stg, g * 2 + (h + 1))
                            pool.sem_inc(s_tick, 1)
                            scatter(h)

        rows1 = 125
        group(0, src.rearrange("(p c) -> p c", p=rows1), dst.rearrange("(p c) -> p c", p=rows1),
              rows1, E1 // rows1, S1, True)
        end_phase()
        group(1, edges2[0].rearrange("(p c) -> p c", p=P), edges2[1].rearrange("(p c) -> p c", p=P),
              P, E2 // P, S2, False)
        end_phase()

        s_x, s_xm, s_t0, s_tw = sem("x_in"), sem("x_tail_cleared"), sem("t0_done"), sem("t0_out")
        s_n, s_sqr = sem("norm_chain"), sem("std_done")

        def moments(link, ready):
            link(nc.vector.tensor_tensor(mv[:, :, 0], stats[:, :, 1], stats[:, :, 4], ALU.add))
            link(nc.vector.tensor_tensor(mv[:, :, 1], stats[:, :, 1], stats[:, :, 4], ALU.subtract))
            link(nc.vector.tensor_scalar(mv[:, :, 0], mv[:, :, 0], 0.5, None, ALU.mult))
            link(nc.vector.scalar_tensor_tensor(mv[:, :, 1], mv[:, :, 1], 0.25, mv[:, :, 1], ALU.mult, ALU.mult))
            link(nc.vector.tensor_tensor(stats[:, :, 0], stats[:, :, 2], stats[:, :, 5], ALU.add))
            link(nc.vector.scalar_tensor_tensor(mv[:, :, 1], stats[:, :, 0], 1.0 / D, mv[:, :, 1],
                                                ALU.mult, ALU.add))
            link.eng.sem_inc(ready, 1)

        with nc.Block() as block:
            s_st, s_ag = sem("stats0"), sem("stats0_all")

            @block.sync
            def _(sp):
                sp.wait_ge(s_xm, 1)
                sp.dma_start(acc[:, 0:(NB - 1) * D].rearrange("p (b f) -> p b f", f=D),
                             x[0:(NB - 1) * P].rearrange("(b p) f -> p b f", p=P)).then_inc(s_x, 16)
                sp.dma_start(acc[0:TAIL, (NB - 1) * D:NB * D], x[(NB - 1) * P:N]).then_inc(s_x, 16)
                sp.wait_ge(s_t0, NB)
                sp.dma_start(table.rearrange("(b p) f -> p b f", p=P),
                             acc[:].rearrange("p (b f) -> p b f", f=D)).then_inc(s_tw, 16)
                sp.wait_ge(s_tw, 16)

            @block.vector
            def _(dve):
                link = Chain(dve, s_n)
                nc.vector.memset(acc[:, (NB - 1) * D:NB * D], 0.0).then_inc(s_xm, 1)
                dve.wait_ge(s_x, 32)
                with dve.Fori(0, NB) as b:
                    nc.vector.bn_stats(stats[:, bass.ds(b, 1)].rearrange("p a s -> p (a s)"),
                                       acc[:, bass.ds(b * D, D)]).then_inc(s_st, 1)
                dve.wait_ge(s_st, NB)
                moments(link, s_ag)
                dve.wait_ge(s_sqr, 1)
                link(nc.vector.reciprocal(rstd[:], rstd[:]))
                link(nc.vector.tensor_tensor(rstd[:], rstd[:], dinv[:], ALU.mult))
                with dve.Fori(0, NB) as b:
                    nc.vector.tensor_scalar(acc[:, bass.ds(b * D, D)], acc[:, bass.ds(b * D, D)],
                                            mv[:, bass.ds(b, 1), 0], rstd[:, bass.ds(b, 1)],
                                            ALU.subtract, ALU.mult).then_inc(s_t0, 1)

            @block.scalar
            def _(act):
                act.wait_ge(s_ag, 1)
                nc.scalar.activation(rstd[:], mv[:, :, 1], ACT.Sqrt, bias=eps[:, 0:1]).then_inc(s_sqr, 1)

        end_phase()

        ring = work[:].rearrange("p (h u f) -> p h u f", h=2, u=U)
        G1 = S1 // (2 * U)
        Q = 4

        def aggregate(l):
            n = f"_l{l}"
            s_row = [sem(f"rows_in{h}" + n) for h in range(2)]
            s_stg, s_tick = sem("indices_staged" + n), sem("pool_tick" + n)
            s_used = sem("ring_half_used" + n)
            s_hot, s_mm, s_add, s_sum = sem("onehots" + n), sem("products" + n), sem("adds" + n), sem("psum_free" + n)
            with nc.Block() as block:
                @block.gpsimd
                def _(pool):
                    with pool.Fori(0, G1) as g:
                        for h in range(2):
                            pool.wait_ge(s_used, g * 2 + (h + 1))
                            pool.sem_inc(s_tick, 1)
                            nc.gpsimd.tensor_copy(stage[:, h], idx[0][:, bass.ds(g * (2 * U) + h * U, U)]).then_inc(s_stg, 1)
                            pool.wait_ge(s_stg, g * 2 + (h + 1))
                            pool.sem_inc(s_tick, 1)
                            for k in range(U):
                                nc.gpsimd.indirect_dma_start(
                                    out=ring[:, h, k], out_offset=None, in_=table,
                                    in_offset=bass.IndirectOffsetOnAxis(ap=stage[:, h, k:k + 1], axis=0),
                                ).then_inc(s_row[h], 16)

                @block.tensor
                def _(pe):
                    pe.sem_inc(s_used, 2)
                    with pe.Fori(0, G1) as g:
                        for h in range(2):
                            pe.wait_ge(s_row[h], (g + 1) * (16 * U))
                            pe.wait_ge(s_hot, g * 2 + (h + 1))
                            for k in range(U):
                                bank = (k // 2) % 8
                                if k % Q == 0:
                                    pe.wait_ge(s_sum, g * (2 * U // Q) + (h * U + k) // Q + 1)
                                mm = nc.tensor.matmul(ps[:, bank, (k % 2) * D:(k % 2 + 1) * D], onehot[:, h, k],
                                                      ring[:, h, k], start=True, stop=True, skip_group_check=True)
                                if k % Q == Q - 1:
                                    mm.then_inc(s_mm, 1)
                            pe.wait_ge(s_mm, g * (2 * U // Q) + (h + 1) * (U // Q))
                            pe.sem_inc(s_used, 1)

                @block.vector
                def _(dve):
                    dve.sem_inc(s_sum, U // Q)
                    def hots(g, h):
                        nc.vector.tensor_tensor(
                            onehot[:, h], iota[:].unsqueeze(1).broadcast_to([P, U, P]),
                            dloc[0][:, bass.ds(g * (2 * U) + h * U, U)].unsqueeze(2).broadcast_to([P, U, P]),
                            ALU.is_equal).then_inc(s_hot, 1)
                    with dve.Fori(0, G1) as g:
                        for h in range(2):
                            dve.wait_ge(s_used, g * 2 + (h + 1))
                            hots(g, h)
                            for k in range(U):
                                bank = (k // 2) % 8
                                s = g * (2 * U) + (h * U + k)
                                b = dve.value_load(blk[0][0:1, bass.ds(s, 1)], min_val=0, max_val=NB - 1)
                                if k % Q == 0:
                                    dve.wait_ge(s_mm, g * (2 * U // Q) + (h * U + k) // Q + 1)
                                at = bass.ds(b * D, D)
                                nc.vector.tensor_tensor(acc[:, at], acc[:, at], ps[:, bank, (k % 2) * D:(k % 2 + 1) * D],
                                                        ALU.add).then_inc(s_add, 1)
                                dve.wait_ge(s_add, s + 1)
                                if k % Q == Q - 1:
                                    dve.sem_inc(s_sum, 1)

        zst = work[:, 0:2 * D].rearrange("p (a f) -> p a f", a=2)
        zt = work[:, 2 * D:4 * D].rearrange("p (a f) -> p a f", a=2)
        ust = work[:, 4 * D:6 * D].rearrange("p (a f) -> p a f", a=2)
        xin = work[:, 6 * D:8 * D].rearrange("p (a f) -> p a f", a=2)

        def finish(l):
            last = l == 2
            n = f"_f{l}"
            s_z, s_zp, s_zt, s_y, s_u, s_a, s_o = (sem(c + n) for c in (
                "scaled", "transposed", "transposed_copied", "weighted", "activated", "block_done", "block_out"))
            s_xi = [sem(f"x_in{a}" + n) for a in range(2)]
            with nc.Block() as block:
                @block.scalar
                def _(act):
                    with act.Fori(0, PAIRS) as g:
                        for a in range(2):
                            b = g * 2 + a
                            if last:
                                act.wait_ge(s_zt, g * 2 + a) if False else None
                            nc.scalar.activation(zst[:, a], acc[:, bass.ds(b * D, D)], ACT.Copy,
                                                 scale=dinv[:, bass.ds(b, 1)]).then_inc(s_z, 1)
                        for a in range(2):
                            act.wait_ge(s_y, g * 2 + (a + 1))
                            if not last:
                                nc.scalar.activation(ust[:, a], ps[:, 2 + a, 0:D], ACT.Gelu_apprx_tanh).then_inc(s_u, 1)
                            else:
                                nc.scalar.copy(ust[:, a], ps[:, 2 + a, 0:D]).then_inc(s_u, 1)
                            act.wait_ge(s_a, g * 2 + (a + 1))

                @block.tensor
                def _(pe):
                    with pe.Fori(0, PAIRS) as g:
                        for a in range(2):
                            pe.wait_ge(s_z, g * 2 + (a + 1))
                            for k in range(KD):
                                mm = nc.tensor.transpose(ps[:, a, k * P:(k + 1) * P], zst[:, a, k * P:(k + 1) * P], ident[:])
                            mm.then_inc(s_zp, 1)
                        for a in range(2):
                            pe.wait_ge(s_zt, g * 2 + (a + 1))
                            nc.tensor.matmul(ps[:, 2 + a, 0:D], ones[0:1, :], gb_sb[0:1, l], start=True, stop=False)
                            for k in range(KD):
                                mm = nc.tensor.matmul(ps[:, 2 + a, 0:D], zt[:, a, k * P:(k + 1) * P], gw_sb[:, l, k],
                                                      start=False, stop=(k == KD - 1))
                            mm.then_inc(s_y, 1)

                @block.vector
                def _(dve):
                    with dve.Fori(0, PAIRS) as g:
                        for a in range(2):
                            dve.wait_ge(s_zp, g * 2 + (a + 1))
                            nc.vector.tensor_copy(zt[:, a], ps[:, a, 0:D]).then_inc(s_zt, 1)
                        for a in range(2):
                            b = g * 2 + a
                            dve.wait_ge(s_u, g * 2 + (a + 1))
                            if not last:
                                nc.vector.tensor_scalar(acc[:, bass.ds(b * D, D)], ust[:, a], dinv[:, bass.ds(b, 1)],
                                                        None, ALU.mult).then_inc(s_a, 1)
                            else:
                                dve.wait_ge(s_xi[a], (g + 1) * 16)
                                nc.vector.tensor_tensor(acc[:, bass.ds(b * D, D)], ust[:, a], xin[:, a],
                                                        ALU.add).then_inc(s_a, 1)

                @block.sync
                def _(sp):
                    dest = x1_dram if last else table
                    if last:
                        sp.dma_start(xin[:, 0], x[0:P]).then_inc(s_xi[0], 16)
                        sp.dma_start(xin[:, 1], x[P:2 * P]).then_inc(s_xi[1], 16)
                    def store(b, a, more):
                        hold(sp, s_a, b + 1)
                        sp.dma_start(dest[bass.ds(b * P, P)], acc[:, bass.ds(b * D, D)]).then_inc(s_o, 16)
                        if last and more:
                            sp.dma_start(xin[:, a], x[bass.ds((b + 2) * P, P)]).then_inc(s_xi[a], 16)
                    with sp.Fori(0, PAIRS - 2) as g:
                        for a in range(2):
                            store(g * 2 + a, a, True)
                    store(NB - 4, 0, True)
                    store(NB - 3, 1, False)
                    if last:
                        sp.dma_start(xin[0:TAIL, 1], x[(NB - 1) * P:N]).then_inc(s_xi[1], 16)
                    for a in range(2):
                        b = NB - 2 + a
                        sp.wait_ge(s_a, b + 1)
                        sp.dma_start(dest[b * P:(b + 1) * P], acc[:, b * D:(b + 1) * D]).then_inc(s_o, 16)
                    sp.wait_ge(s_o, 16 * NB)

        for l in range(3):
            aggregate(l)
            finish(l)
            end_phase()

        s_st, s_ag, s_sqr, s_n = sem("stats1"), sem("stats1_all"), sem("std1_done"), sem("chain1")
        s_xn, s_xp, s_xt, s_h, s_hc, s_xo = (sem(c) for c in (
            "xn", "xn_transposed", "xn_t_copied", "h_done", "h_copied", "xn_t_out"))
        s_g, s_go = sem("gat_rows"), sem("gat_table_out")
        h16 = HG[:, :, 0:HE]
        with nc.Block() as block:
            @block.vector
            def _(dve):
                link = Chain(dve, s_n)
                with dve.Fori(0, NB) as b:
                    nc.vector.bn_stats(stats[:, bass.ds(b, 1)].rearrange("p a s -> p (a s)"),
                                       acc[:, bass.ds(b * D, D)]).then_inc(s_st, 1)
                dve.wait_ge(s_st, NB)
                moments(link, s_ag)
                dve.wait_ge(s_sqr, 1)
                link(nc.vector.reciprocal(rstd[:], rstd[:]))
                with dve.Fori(0, PAIRS) as g:
                    for a in range(2):
                        b = g * 2 + a
                        nc.vector.tensor_scalar(zst[:, a], acc[:, bass.ds(b * D, D)],
                                                mv[:, bass.ds(b, 1), 0], rstd[:, bass.ds(b, 1)],
                                                ALU.subtract, ALU.mult).then_inc(s_xn, 1)
                    for a in range(2):
                        b = g * 2 + a
                        dve.wait_ge(s_h, g * 2 + (a + 1))
                        nc.vector.tensor_copy(HG[:, bass.ds(b, 1), 0:HE].rearrange("p a e -> p (a e)"),
                                              ps[:, 2 + a, 0:HE]).then_inc(s_hc, 1)
                dve.wait_ge(s_hc, NB)
                for which, to in ((0, HG[:, :, HE:GW]), (1, ad[:])):
                    link(nc.vector.tensor_tensor(small[:, which], h16, row16[:, which].unsqueeze(1).broadcast_to([P, NB, HE]),
                                                 ALU.mult))
                    link(nc.vector.tensor_reduce(to, small[:, which].rearrange("p b (h e) -> p b h e", e=NE), AX.X, ALU.add))
                nc.vector.tensor_copy(emx[:], HG[:, :, HE:GW]).then_inc(s_g, 1)

            @block.scalar
            def _(act):
                act.wait_ge(s_ag, 1)
                nc.scalar.activation(rstd[:], mv[:, :, 1], ACT.Sqrt, bias=eps[:, 0:1]).then_inc(s_sqr, 1)
                with act.Fori(0, PAIRS) as g:
                    for a in range(2):
                        act.wait_ge(s_xp, g * 2 + (a + 1))
                        act.wait_ge(s_xo, g * 32 + 16 * a + 16)
                        nc.scalar.copy(zt[:, a], ps[:, a, 0:D]).then_inc(s_xt, 1)

            @block.tensor
            def _(pe):
                with pe.Fori(0, PAIRS) as g:
                    for a in range(2):
                        pe.wait_ge(s_xn, g * 2 + (a + 1))
                        for k in range(KD):
                            mm = nc.tensor.transpose(ps[:, a, k * P:(k + 1) * P], zst[:, a, k * P:(k + 1) * P], ident[:])
                        mm.then_inc(s_xp, 1)
                    for a in range(2):
                        pe.wait_ge(s_xt, g * 2 + (a + 1))
                        for k in range(KD):
                            mm = nc.tensor.matmul(ps[:, 2 + a, 0:HE], zt[:, a, k * P:(k + 1) * P], wg_sb[:, k],
                                                  start=(k == 0), stop=(k == KD - 1))
                        mm.then_inc(s_h, 1)

            @block.sync
            def _(sp):
                sp.sem_inc(s_xo, 32)
                with sp.Fori(0, PAIRS) as g:
                    for a in range(2):
                        hold(sp, s_xt, g * 2 + (a + 1))
                        sp.dma_start(xnt_dram[bass.ds(g * 2 + a, 1)].rearrange("a p f -> (a p) f"), zt[:, a]).then_inc(s_xo, 16)
                        hold(sp, s_xo, g * 32 + (16 * a + 48))
                sp.wait_ge(s_g, 1)
                sp.dma_start(gat_table.rearrange("(b p) f -> p b f", p=P), HG[:]).then_inc(s_go, 16)
                sp.wait_ge(s_go, 16)

        end_phase()

        G2 = S2 // (2 * U)
        grow = work[:, 0:2 * U * GW].rearrange("p (h u f) -> p h u f", h=2, u=U)
        penal = work[:, 1024:1024 + U * P].bitcast(BF16).rearrange("p (h u m) -> p h u m", h=2, u=U)
        mx = work[:, 4096:4096 + 2 * U * NH].rearrange("p (h u k) -> p h u k", h=2, u=U)
        rows_kept = acc[:, 0:S2 * GW]
        s_row = [sem(f"gat_rows_in{h}") for h in range(2)]
        s_stg, s_tick, s_used = sem("gat_staged"), sem("gat_tick"), sem("gat_half_used")
        s_hot, s_mm, s_red, s_mrg, s_keep = sem("gat_penalties"), sem("gat_scores"), sem("gat_reduced"), sem("gat_merged"), sem("gat_rows_kept")
        s_pf = sem("gat_psum_free")
        s_c2 = sem("gat_chain")
        with nc.Block() as block:
            @block.gpsimd
            def _(pool):
                with pool.Fori(0, G2) as g:
                    for h in range(2):
                        pool.wait_ge(s_used, g * 2 + (h + 1))
                        pool.sem_inc(s_tick, 1)
                        pool.wait_ge(s_keep, g * 2 + (h + 1))
                        pool.sem_inc(s_tick, 1)
                        nc.gpsimd.tensor_copy(stage[:, h], idx[1][:, bass.ds(g * (2 * U) + h * U, U)]).then_inc(s_stg, 1)
                        pool.wait_ge(s_stg, g * 2 + (h + 1))
                        pool.sem_inc(s_tick, 1)
                        for k in range(U):
                            nc.gpsimd.indirect_dma_start(
                                out=grow[:, h, k], out_offset=None, in_=gat_table,
                                in_offset=bass.IndirectOffsetOnAxis(ap=stage[:, h, k:k + 1], axis=0),
                            ).then_inc(s_row[h], 16)

            @block.scalar
            def _(act):
                act.sem_inc(s_keep, 2)
                with act.Fori(0, G2) as g:
                    for h in range(2):
                        act.wait_ge(s_row[h], (g + 1) * (16 * U))
                        nc.scalar.copy(rows_kept[:, bass.ds((g * (2 * U) + h * U) * GW, U * GW)],
                                       grow[:, h].rearrange("p u f -> p (u f)")).then_inc(s_keep, 1)

            @block.tensor
            def _(pe):
                pe.sem_inc(s_used, 2)
                with pe.Fori(0, G2) as g:
                    for h in range(2):
                        pe.wait_ge(s_row[h], (g + 1) * (16 * U))
                        pe.wait_ge(s_hot, g * 2 + (h + 1))
                        for k in range(U):
                            pe.wait_ge(s_pf, g * (2 * U) + (h * U + k + 1))
                            bank = k % 8
                            for j in range(NH):
                                nc.tensor.matmul(ps[:, bank, j * P:(j + 1) * P], penal[:, h, k], ident_bf[:],
                                                 start=(j == 0), stop=False, skip_group_check=True)
                            for j in range(NH):
                                mm = nc.tensor.matmul(ps[:, bank, j * P:(j + 1) * P],
                                                      grow[:, h, k, HE + j:HE + j + 1].broadcast_to([P, P]), ident[:],
                                                      start=False, stop=(j == NH - 1), skip_group_check=True)
                            mm.then_inc(s_mm, 1)
                        pe.wait_ge(s_mm, g * (2 * U) + (h + 1) * U)
                        pe.sem_inc(s_used, 1)

            @block.vector
            def _(dve):
                dve.sem_inc(s_pf, 8)
                with dve.Fori(0, G2) as g:
                    for h in range(2):
                        dve.wait_ge(s_used, g * 2 + (h + 1))
                        nc.vector.tensor_tensor(
                            onehot[:, h], iota[:].unsqueeze(1).broadcast_to([P, U, P]),
                            dloc[1][:, bass.ds(g * (2 * U) + h * U, U)].unsqueeze(2).broadcast_to([P, U, P]),
                            ALU.not_equal).then_inc(s_c2, 1)
                        dve.wait_ge(s_c2, g * 2 + (h + 1))
                        nc.vector.tensor_scalar(penal[:, h], onehot[:, h], BIG, None, ALU.mult).then_inc(s_hot, 1)
                        for k in range(U):
                            dve.wait_ge(s_mm, g * (2 * U) + (h * U + k + 1))
                            nc.vector.tensor_reduce(mx[:, h, k], ps[:, k % 8].rearrange("p (j e) -> p j e", j=NH),
                                                    AX.X, ALU.max).then_inc(s_red, 1)
                            dve.wait_ge(s_red, g * (2 * U) + (h * U + k + 1))
                            dve.sem_inc(s_pf, 1)
                            s = g * (2 * U) + (h * U + k)
                            b = dve.value_load(blk[1][0:1, bass.ds(s, 1)], min_val=0, max_val=NB - 1)
                            to = emx[:, bass.ds(b, 1)].rearrange("p a k -> p (a k)")
                            nc.vector.tensor_tensor(to, to, mx[:, h, k], ALU.max).then_inc(s_mrg, 1)
                            dve.wait_ge(s_mrg, s + 1)

        end_phase()

        s_e, s_ee, s_eo = sem("self_scores"), sem("self_exp"), sem("self_chain")
        sc = small[:, 2, :, 0:NH]
        sc2 = small[:, 2, :, NH:2 * NH]
        with nc.Block() as block:
            @block.vector
            def _(dve):
                link = Chain(dve, s_eo)
                link(nc.vector.tensor_tensor(sc, emx[:], ad[:], ALU.add))
                link(nc.vector.scalar_tensor_tensor(V[:, :, NH:2 * NH], sc, 0.2, sc, ALU.mult, ALU.max))
                link(nc.vector.tensor_copy(V[:, :, 0:NH], ad[:]))
                link(nc.vector.tensor_tensor(sc, HG[:, :, HE:GW], ad[:], ALU.add))
                link(nc.vector.scalar_tensor_tensor(sc2, sc, 0.2, sc, ALU.mult, ALU.max))
                link(nc.vector.tensor_tensor(sc, sc2, V[:, :, NH:2 * NH], ALU.subtract))
                dve.sem_inc(s_e, 1)
                dve.wait_ge(s_ee, 1)
                link(nc.vector.tensor_copy(AGG[:, :, HE:GW], sc2))
                for j in range(NH):
                    link(nc.vector.tensor_tensor(AGG[:, :, j * NE:(j + 1) * NE], HG[:, :, j * NE:(j + 1) * NE],
                                                 sc2[:, :, j:j + 1].broadcast_to([P, NB, NE]), ALU.mult))

            @block.scalar
            def _(act):
                act.wait_ge(s_e, 1)
                nc.scalar.activation(sc2, sc, ACT.Exp).then_inc(s_ee, 1)

        end_phase()

        oht = work[:, 0:U * P].rearrange("p (u m) -> p u m", u=U)
        msg = work[:, U * P:U * P + 2 * U * GW].rearrange("p (h u f) -> p h u f", h=2, u=U)
        sc3 = work[:, 4096:4096 + 3 * U * NH].rearrange("p (a u k) -> p a u k", a=3, u=U)
        kept = rows_kept.rearrange("p (s f) -> p s f", f=GW)
        (s_hot, s_tp, s_tc, s_dist, s_sc, s_ex, s_msg, s_mm, s_add, s_c3, s_pf) = (sem("b2_" + c) for c in (
            "onehots", "transposed", "transposed_copied", "distributed", "scores", "exps", "messages", "products", "adds",
            "chain", "psum_free"))
        with nc.Block() as block:
            @block.vector
            def _(dve):
                with dve.Fori(0, G2) as g:
                    for h in range(2):
                        at = bass.ds(g * (2 * U) + h * U, U)
                        nc.vector.tensor_tensor(
                            onehot[:, h], iota[:].unsqueeze(1).broadcast_to([P, U, P]),
                            dloc[1][:, at].unsqueeze(2).broadcast_to([P, U, P]), ALU.is_equal).then_inc(s_hot, 1)
                        dve.wait_ge(s_dist, g * 2 + (h + 1))
                        d8 = ps[:, 4, 0:U * 2 * NH].rearrange("p (u f) -> p u f", u=U)
                        nc.vector.tensor_tensor(sc3[:, 0], kept[:, at, HE:GW], d8[:, :, 0:NH], ALU.add).then_inc(s_c3, 1)
                        c = g * 6 + 3 * h
                        dve.wait_ge(s_c3, c + 1)
                        nc.vector.scalar_tensor_tensor(sc3[:, 1], sc3[:, 0], 0.2, sc3[:, 0], ALU.mult, ALU.max).then_inc(s_c3, 1)
                        dve.wait_ge(s_c3, c + 2)
                        nc.vector.tensor_tensor(sc3[:, 0], sc3[:, 1], d8[:, :, NH:2 * NH], ALU.subtract).then_inc(s_c3, 1)
                        dve.wait_ge(s_c3, c + 3)
                        nc.vector.tensor_scalar(sc3[:, 2], sc3[:, 0], 0.0, None, ALU.min).then_inc(s_sc, 1)
                        dve.wait_ge(s_ex, g * 2 + (h + 1))
                        for j in range(NH):
                            mul = nc.vector.tensor_tensor(msg[:, h, :, j * NE:(j + 1) * NE], kept[:, at, j * NE:(j + 1) * NE],
                                                          msg[:, h, :, HE + j:HE + j + 1].broadcast_to([P, U, NE]), ALU.mult)
                        mul.then_inc(s_msg, 1)
                        dve.wait_ge(s_mm, g * 2 + (h + 1))
                        for k in range(U):
                            s = g * (2 * U) + (h * U + k)
                            b = dve.value_load(blk[1][0:1, bass.ds(s, 1)], min_val=0, max_val=NB - 1)
                            to = AGG[:, bass.ds(b, 1)].rearrange("p a k -> p (a k)")
                            nc.vector.tensor_tensor(to, to, ps[:, 5, k * GW:(k + 1) * GW], ALU.add).then_inc(s_add, 1)
                            dve.wait_ge(s_add, s + 1)

            @block.tensor
            def _(pe):
                with pe.Fori(0, G2) as g:
                    for h in range(2):
                        pe.wait_ge(s_hot, g * 2 + (h + 1))
                        for k in range(U):
                            mm = nc.tensor.transpose(ps[:, k // 4, (k % 4) * P:(k % 4 + 1) * P], onehot[:, h, k], ident[:])
                        mm.then_inc(s_tp, 1)
                        pe.wait_ge(s_tc, g * 2 + (h + 1))
                        for k in range(U):
                            s = g * (2 * U) + (h * U + k)
                            b = pe.value_load(blk[1][0:1, bass.ds(s, 1)], min_val=0, max_val=NB - 1)
                            mm = nc.tensor.matmul(ps[:, 4, k * 2 * NH:(k + 1) * 2 * NH], oht[:, k],
                                                  V[:, bass.ds(b, 1)].rearrange("p a k -> p (a k)"),
                                                  start=True, stop=True, skip_group_check=True)
                        mm.then_inc(s_dist, 1)
                        pe.wait_ge(s_msg, g * 2 + (h + 1))
                        for k in range(U):
                            mm = nc.tensor.matmul(ps[:, 5, k * GW:(k + 1) * GW], onehot[:, h, k], msg[:, h, k],
                                                  start=True, stop=True, skip_group_check=True)
                        mm.then_inc(s_mm, 1)

            @block.scalar
            def _(act):
                with act.Fori(0, G2) as g:
                    for h in range(2):
                        act.wait_ge(s_tp, g * 2 + (h + 1))
                        nc.scalar.copy(oht.rearrange("p u m -> p (u m)"), ps[:, 0:4].rearrange("p a f -> p (a f)")).then_inc(s_tc, 1)
                        act.wait_ge(s_sc, g * 2 + (h + 1))
                        nc.scalar.activation(msg[:, h, :, HE:GW], sc3[:, 2], ACT.Exp).then_inc(s_ex, 1)

        end_phase()

        s_r, s_rs, s_re, s_rv = sem("route_chain"), sem("route_std"), sem("route_exp"), sem("route_var")
        a16 = small[:, 0]
        t16 = small[:, 1]
        u16 = small[:, 2]
        with nc.Block() as block:
            @block.vector
            def _(dve):
                link = Chain(dve, s_r)
                link(nc.vector.tensor_scalar(emx[:], AGG[:, :, HE:GW], 1e-16, None, ALU.add))
                link(nc.vector.reciprocal(emx[:], emx[:]))
                for j in range(NH):
                    link(nc.vector.tensor_tensor(a16[:, :, j * NE:(j + 1) * NE], AGG[:, :, j * NE:(j + 1) * NE],
                                                 emx[:, :, j:j + 1].broadcast_to([P, NB, NE]), ALU.mult))
                row = lambda i: row16[:, i].unsqueeze(1).broadcast_to([P, NB, HE])
                link(nc.vector.tensor_tensor(t16, a16, row(2), ALU.add))
                m = mv[:, :, 0:1]
                link(nc.vector.tensor_reduce(mv[:, :, 0], t16, AX.X, ALU.add))
                link(nc.vector.tensor_scalar(mv[:, :, 1], mv[:, :, 0], 1.0 / HE, None, ALU.mult))
                link(nc.vector.tensor_tensor(a16, t16, mv[:, :, 1:2].broadcast_to([P, NB, HE]), ALU.subtract))
                link(nc.vector.tensor_tensor(t16, a16, a16, ALU.mult))
                link(nc.vector.tensor_reduce(mv[:, :, 0], t16, AX.X, ALU.add))
                dve.sem_inc(s_rv, 1)
                dve.wait_ge(s_rs, 1)
                link(nc.vector.reciprocal(rstd[:], rstd[:]))
                link(nc.vector.tensor_tensor(t16, a16, rstd[:].unsqueeze(2).broadcast_to([P, NB, HE]), ALU.mult))
                link(nc.vector.tensor_tensor(a16, t16, row(3), ALU.mult))
                link(nc.vector.tensor_tensor(t16, a16, row(4), ALU.add))
                link(nc.vector.tensor_reduce(gates[:], t16.rearrange("p b (h e) -> p b e h", e=NE), AX.X, ALU.add))
                link(nc.vector.tensor_scalar(gates[:], gates[:], 1.0 / NH, None, ALU.mult))
                wins = u16[:, :, 0:NE]
                beat = u16[:, :, NE:NE + 1]
                link(nc.vector.memset(u16, 0.0))
                for lo in range(NE):
                    for hi in range(lo + 1, NE):
                        link(nc.vector.tensor_tensor(beat, gates[:, :, lo:lo + 1], gates[:, :, hi:hi + 1], ALU.is_ge))
                        link(nc.vector.tensor_tensor(wins[:, :, lo:lo + 1], wins[:, :, lo:lo + 1], beat, ALU.add))
                        link(nc.vector.tensor_tensor(beat, gates[:, :, lo:lo + 1], gates[:, :, hi:hi + 1], ALU.is_lt))
                        link(nc.vector.tensor_tensor(wins[:, :, hi:hi + 1], wins[:, :, hi:hi + 1], beat, ALU.add))
                link(nc.vector.tensor_reduce(mv[:, :, 1], gates[:], AX.X, ALU.max))
                ex = u16[:, :, 2 * NE:3 * NE]
                link(nc.vector.tensor_tensor(ex, gates[:], mv[:, :, 1:2].broadcast_to([P, NB, NE]), ALU.subtract))
                dve.sem_inc(s_rv, 1)
                dve.wait_ge(s_re, 1)
                link(nc.vector.scalar_tensor_tensor(ex, wins, float(NE - 2), gates[:], ALU.is_ge, ALU.mult))
                link(nc.vector.tensor_reduce(mv[:, :, 0], ex, AX.X, ALU.add))
                link(nc.vector.reciprocal(rstd[:], mv[:, :, 0]))
                link(nc.vector.tensor_tensor(gates[:], ex, rstd[:].unsqueeze(2).broadcast_to([P, NB, NE]), ALU.mult))

            @block.scalar
            def _(act):
                act.wait_ge(s_rv, 1)
                nc.scalar.activation(rstd[:], mv[:, :, 0], ACT.Sqrt, bias=eps[:, 0:1], scale=1.0 / HE).then_inc(s_rs, 1)
                act.wait_ge(s_rv, 2)
                nc.scalar.activation(gates[:], u16[:, :, 2 * NE:3 * NE], ACT.Exp).then_inc(s_re, 1)

        end_phase()

        o = 0

        def part(n):
            nonlocal o
            v = acc[:, o:o + n]
            o += n
            return v
        w1 = part(NE * KD * HID).rearrange("p (e k n) -> p e k n", e=NE, k=KD)
        w2 = part(NE * KH * D).rearrange("p (e k n) -> p e k n", e=NE, k=KH)
        b1 = part(NE * KH).rearrange("p (e k) -> p e k", e=NE)
        b2 = part(NE * D).rearrange("p (e n) -> p e n", e=NE)
        xt = part(2 * 2 * D).rearrange("p (r a k n) -> p r a k n", r=2, a=2, k=KD)
        hid = part(2 * KH * 2 * P).rearrange("p (r k n) -> p r k n", r=2, k=KH)
        ysum = part(2 * 2 * D).rearrange("p (r a f) -> p r a f", r=2, a=2)
        s_ew = sem("expert_weights")
        s_xt = [sem(f"xn_t_in{r}") for r in range(2)]
        s_x1 = [sem(f"x1_in{r}") for r in range(2)]
        s_up, s_gl, s_dn, s_yc, s_done, s_out = (sem(c) for c in (
            "up_done", "gelu_done", "down_done", "expert_added", "pair_done", "rows_out"))
        with nc.Block() as block:
            @block.sync
            def _(sp):
                sp.dma_start(w1, ew1.rearrange("e (k p) n -> p e k n", p=P)).then_inc(s_ew, 16)
                sp.dma_start(w2, ew2.rearrange("e (k p) n -> p e k n", p=P)).then_inc(s_ew, 16)
                sp.dma_start(b1, eb1.rearrange("e (k p) -> p e k", p=P), allow_slow_non_contiguous=True).then_inc(s_ew, 16)
                sp.dma_start(b2[0:1], eb2.rearrange("(a e) n -> a e n", a=1)).then_inc(s_ew, 16)

                def loads(g, r):
                    sp.dma_start(xt[:, r].rearrange("p a k n -> p a (k n)"),
                                 xnt_dram[bass.ds(g * 2, 2)].rearrange("a p f -> p a f")).then_inc(s_xt[r], 16)
                    sp.dma_start(ysum[:, r], x1_dram[bass.ds(g * 2 * P, 2 * P)].rearrange(
                        "(a p) f -> p a f", p=P)).then_inc(s_x1[r], 16)
                loads(0, 0)
                loads(1, 1)
                def store(g, r, more):
                    hold(sp, s_done, g + 1)
                    sp.dma_start(out[bass.ds(g * 2 * P, 2 * P)].rearrange("(a p) f -> p a f", p=P),
                                 ysum[:, r]).then_inc(s_out, 16)
                    hold(sp, s_out, g * 16 + 16)
                    if more:
                        loads(g + 2, r)
                with sp.Fori(0, (PAIRS - 3) // 2) as q:
                    for r in range(2):
                        store(q * 2 + r, r, True)
                store(PAIRS - 3, 0, True)
                store(PAIRS - 2, 1, False)
                g = PAIRS - 1
                sp.wait_ge(s_done, PAIRS)
                sp.dma_start(out[g * 2 * P:g * 2 * P + P], ysum[:, 0, 0]).then_inc(s_out, 16)
                sp.dma_start(out[g * 2 * P + P:N], ysum[0:TAIL, 0, 1]).then_inc(s_out, 16)
                sp.wait_ge(s_out, 16 * (PAIRS + 1))

            def pairs(eng, body):
                with eng.Fori(0, (PAIRS - 1) // 2) as q:
                    for r in range(2):
                        body(q * 2 + r, r, q + 1)
                body(PAIRS - 1, 0, (PAIRS - 1) // 2 + 1)

            @block.tensor
            def _(pe):
                pe.wait_ge(s_ew, 64)

                def body(g, r, uses):
                    pe.wait_ge(s_xt[r], uses * 16)
                    for e in range(NE):
                        pe.wait_ge(s_gl, g * NE + (e + 1))
                        for m in range(KH):
                            for a in range(2):
                                for k in range(KD):
                                    mm = nc.tensor.matmul(
                                        ps[:, 2 * (e % 2) + m // 2, (m % 2) * 2 * P + a * P:(m % 2) * 2 * P + (a + 1) * P],
                                        w1[:, e, k, m * P:(m + 1) * P], xt[:, r, a, k],
                                        start=(k == 0), stop=(k == KD - 1), skip_group_check=True)
                        mm.then_inc(s_up, 1)
                        if e > 0:
                            down(g, e - 1)
                    down(g, NE - 1)

                def down(g, e):
                    pe.wait_ge(s_gl, g * NE + (e + 3))
                    pe.wait_ge(s_yc, g * NE + (e + 1))
                    for a in range(2):
                        to = ps[:, 4 + e % 2, a * D:(a + 1) * D]
                        nc.tensor.matmul(to, ones[0:1, :], b2[0:1, e], start=True, stop=False, skip_group_check=True)
                        for m in range(KH):
                            mm = nc.tensor.matmul(to, hid[:, e % 2, m, a * P:(a + 1) * P], w2[:, e, m],
                                                  start=False, stop=(m == KH - 1), skip_group_check=True)
                    mm.then_inc(s_dn, 1)
                pairs(pe, body)

            @block.scalar
            def _(act):
                act.sem_inc(s_gl, 2)

                def body(g, r, uses):
                    for e in range(NE):
                        act.wait_ge(s_up, g * NE + (e + 1))
                        if True:
                            act.wait_ge(s_dn, g * NE + (e + 1))
                        for m in range(KH):
                            ge = nc.scalar.activation(hid[:, e % 2, m], ps[:, 2 * (e % 2) + m // 2, (m % 2) * 2 * P:(m % 2 + 1) * 2 * P],
                                                      ACT.Gelu, bias=b1[:, e, m:m + 1])
                        ge.then_inc(s_gl, 1)
                pairs(act, body)

            @block.vector
            def _(dve):
                dve.sem_inc(s_yc, 2)
                dve.sem_inc(s_dn, 2)

                def body(g, r, uses):
                    dve.wait_ge(s_x1[r], uses * 16)
                    for e in range(NE):
                        dve.wait_ge(s_dn, g * NE + (e + 3))
                        for a in range(2):
                            add = nc.vector.scalar_tensor_tensor(
                                ysum[:, r, a], ps[:, 4 + e % 2, a * D:(a + 1) * D],
                                gates[:, bass.ds(g * 2 + a, 1), e], ysum[:, r, a], ALU.mult, ALU.add)
                        add.then_inc(s_yc, 1)
                        dve.wait_ge(s_yc, g * NE + (e + 3))
                    dve.sem_inc(s_done, 1)
                pairs(dve, body)


INS = ["x", "src", "dst", "L0_gnn_W1", "L0_gnn_b1", "L0_gnn_W2", "L0_gnn_b2", "L0_gnn_W3", "L0_gnn_b3",
       "L0_ffn_W_gat", "L0_ffn_att_src", "L0_ffn_att_dst", "L0_ffn_b_gat", "L0_ffn_ln_gamma", "L0_ffn_ln_beta",
       "L0_ffn_W1", "L0_ffn_b1", "L0_ffn_W2", "L0_ffn_b2", "L0_ffn_edge_index"]


def kernel(**inputs):
    import numpy as np
    import concourse.bacc as bacc
    from concourse.bass_utils import run_bass_kernel_spmd

    nc = bacc.Bacc("TRN2", target_bir_lowering=False, num_devices=1)
    arrays, a = {}, {}
    for name in INS:
        v = np.ascontiguousarray(inputs[name])
        arrays[name + "_in"] = v
        a[name] = nc.dram_tensor(name + "_in", v.shape, mybir.dt.from_np(v.dtype), kind="ExternalInput").ap()
    out = nc.dram_tensor("out", inputs["x"].shape, F32, kind="ExternalOutput").ap()
    build(nc, a["x"], a["src"], a["dst"], [a[f"L0_gnn_W{i}"] for i in (1, 2, 3)], [a[f"L0_gnn_b{i}"] for i in (1, 2, 3)],
          a["L0_ffn_W_gat"], a["L0_ffn_att_src"], a["L0_ffn_att_dst"], a["L0_ffn_b_gat"], a["L0_ffn_ln_gamma"],
          a["L0_ffn_ln_beta"], a["L0_ffn_W1"], a["L0_ffn_b1"], a["L0_ffn_W2"], a["L0_ffn_b2"],
          a["L0_ffn_edge_index"], out)
    r = run_bass_kernel_spmd(nc, [arrays], core_ids=[0])
    return r.results[0]["out"]
```

```python
from contextlib import ExitStack

import concourse.bass as bass
from concourse import mybir

ALU = mybir.AluOpType
ACT = mybir.ActivationFunctionType
F32 = mybir.dt.float32
BF16 = mybir.dt.bfloat16
I32 = mybir.dt.int32
AX = mybir.AxisListType

P = 128
U = 16
SRC_BITS = 14
NO_DST = 255
BIG = -3.0e38
EPS = 1e-5


def steps_for(edges, blocks):
    unit = P
    need = -(-edges // P) + blocks - 1
    return -(-need // unit) * unit


class Chain:

    def __init__(self, eng, sem):
        self.eng, self.sem, self.n = eng, sem, 0

    def __call__(self, ins):
        ins.then_inc(self.sem, 1)
        self.n += 1
        self.eng.wait_ge(self.sem, self.n)


def build(nc, x, src, dst, gnn_w, gnn_b, w_gat, att_src, att_dst, b_gat, ln_gamma, ln_beta,
          ew1, eb1, ew2, eb2, edges2, out):
    N, D = x.shape
    NB = -(-N // P)
    TAIL = N - (NB - 1) * P
    KD = D // P
    NE, _, HID = ew1.shape
    KH = HID // P
    HE = w_gat.shape[1]
    NH = HE // NE
    GW = HE + NH
    E1, E2 = src.shape[0], edges2.shape[1]
    S1, S2 = steps_for(E1, NB), steps_for(E2, NB)
    PAIRS = NB // 2
    EXT = 32
    assert (S2 + NB) * GW <= NB * D
    assert NB % 2 == 0 and N < 1 << SRC_BITS

    table = nc.dram_tensor("feature_table", (NB * P, D), F32).ap()
    gat_table = nc.dram_tensor("attention_table", (NB * P, GW), F32).ap()
    x1_dram = nc.dram_tensor("x_after_gnn", (NB * P, D), F32).ap()
    xnt_dram = nc.dram_tensor("x_normed_t", (NB, P, KD * P), F32).ap()
    list_dram = [nc.dram_tensor(f"edge_list{i}", (P * s, 1), I32).ap() for i, s in enumerate((S1, S2))]
    blk_dram = [nc.dram_tensor(f"step_block{i}", (s,), I32).ap() for i, s in enumerate((S1, S2))]

    with ExitStack() as ctx:
        def sb(name, shape, dt=F32):
            return ctx.enter_context(nc.sbuf_tensor(name, shape, dt))

        phase_sems = []

        def sem(name):
            s = nc.alloc_semaphore(name=name)
            phase_sems.append(s)
            return s

        def end_phase():
            with nc.Block() as block:
                @block.gpsimd
                def _(pool):
                    for s in phase_sems:
                        pool.sem_clear(s)
            for s in phase_sems:
                nc.release_semaphore(s)
            phase_sems.clear()

        ps = ctx.enter_context(nc.psum_tensor("ps", [P, 8, 512], F32))
        acc = sb("acc", [P, NB * D])
        iota = sb("iota", [P, P])
        ident = sb("ident", [P, P])
        lower = sb("lower", [P, P])
        ones = sb("ones", [P, P])
        zeros = sb("zeros", [P, P])
        step_no = sb("step_no", [P, S1 // P])
        idx = [sb("idx1", [P, S1 + EXT], I32), sb("idx2", [P, S2], I32)]
        dloc = [sb("dloc1", [P, S1 + EXT], BF16), sb("dloc2", [P, S2 + U], BF16)]
        blk = [sb("blk1", [1, S1], I32), sb("blk2", [1, S2], I32)]
        dinv = sb("dinv", [P, NB])
        onehot = sb("onehot", [P, 2, U, P])
        work = sb("work", [P, 2 * U * D])
        stage = sb("stage", [P, 2, U], I32)
        rec_stage = sb("rec_stage", [P, 2, U], I32)
        stats = sb("stats", [P, NB, 6])
        mv = sb("mv", [P, NB, 2])
        rstd = sb("rstd", [P, NB])
        eps = sb("eps", [P, 1])
        gw_sb = sb("gw_sb", [P, 3, KD, D])
        gb_sb = sb("gb_sb", [P, 3, D])
        HG = sb("HG", [P, NB, GW])
        ad = sb("ad", [P, NB, NH])
        emx = sb("emx", [P, NB, NH])
        V = work[:, 4800:4800 + NB * 2 * NH].rearrange("p (b f) -> p b f", f=2 * NH)
        V3 = work[:, 2688:2688 + NB * 3 * NH].bitcast(BF16).rearrange("p (b f c) -> p b f c", f=2 * NH, c=3)
        AGG = acc[:, S2 * GW:(S2 + NB) * GW].rearrange("p (b f) -> p b f", f=GW)
        small = work[:, 2 * U * D - 3 * NB * HE:].rearrange("p (a b e) -> p a b e", a=3, b=NB)
        row16 = sb("row16", [P, 5, HE])
        wg_sb = sb("wg_sb", [P, KD, HE])
        gates = sb("gates", [P, NB, NE])

        node0 = sb("first_node", [P, NB])
        s_held = ctx.enter_context(nc.semaphore("held"))

        def load_blocks(which, i, s, n=8, top=NB - 1):
            _, values = nc.values_load_multi_w_load_instructions(
                blk[i][0:1, bass.ds(s, n)], engines=[which], min_val=0, max_val=top,
                skip_runtime_bounds_check_because="the table counts blocks of the graph, made on the chip")
            return values

        def skewed(eng, count, *stages, period=2):
            lead = -(-max(lag for lag, _ in stages) // period) * period
            loops = (count - lead) // period

            def turn(i):
                for lag, body in stages:
                    if 0 <= i - lag < count:
                        body(i - lag, (i - lag) % period)
            for i in range(lead):
                turn(i)
            with eng.Fori(0, loops) as q:
                for r in range(period):
                    for lag, body in stages:
                        body(q * period + (lead + r - lag), (lead + r - lag) % period)
            for i in range(lead + period * loops, count + lead):
                turn(i)

        def hold(eng, s, value):
            eng.wait_ge(s, value)
            eng.sem_inc(s_held, 1)

        s_c, s_iota = sem("constants_ready"), sem("iota_done")
        s_w = sem("weights_loaded")
        with nc.Block() as block:
            @block.gpsimd
            def _(pool):
                nc.gpsimd.iota(iota[:], pattern=[[1, P]], base=0, channel_multiplier=0,
                               allow_small_or_imprecise_dtypes=True)
                nc.gpsimd.iota(node0[:], pattern=[[P, NB]], base=0, channel_multiplier=0,
                               allow_small_or_imprecise_dtypes=True)
                nc.gpsimd.iota(step_no[:], pattern=[[P, S1 // P]], base=0, channel_multiplier=1,
                               allow_small_or_imprecise_dtypes=True)
                nc.gpsimd.memset(ident[:], 0.0)
                nc.gpsimd.memset(ones[:], 1.0)
                nc.gpsimd.memset(zeros[:], 0.0)
                nc.gpsimd.memset(eps[:], EPS)
                nc.gpsimd.memset(lower[:], 1.0).then_inc(s_iota, 1)
                pool.wait_ge(s_iota, 1)
                nc.gpsimd.affine_select(out=ident[:], in_=ident[:], compare_op=ALU.not_equal, fill=1.0,
                                        base=0, pattern=[[-1, P]], channel_multiplier=1)
                nc.gpsimd.affine_select(out=lower[:], in_=lower[:], compare_op=ALU.is_gt, fill=0.0,
                                        base=0, pattern=[[1, P]], channel_multiplier=-1).then_inc(s_c, 1)

            @block.sync
            def _(sp):
                for i in range(3):
                    sp.dma_start(gw_sb[:, i], gnn_w[i].rearrange("(k p) n -> p k n", p=P)).then_inc(s_w, 16)
                    sp.dma_start(gb_sb[:, i], gnn_b[i].rearrange("(a n) -> a n", a=1).broadcast_to([P, D])).then_inc(s_w, 16)
                sp.dma_start(wg_sb[:], w_gat.rearrange("(k p) n -> p k n", p=P)).then_inc(s_w, 16)
                for i, v in enumerate((att_src.rearrange("h e -> (h e)"), att_dst.rearrange("h e -> (h e)"),
                                       b_gat, ln_gamma, ln_beta)):
                    sp.dma_start(row16[:, i], v.rearrange("(a n) -> a n", a=1).broadcast_to([P, HE])).then_inc(s_w, 16)
                sp.wait_ge(s_w, 16 * 12)

        q_tab = sb("first_step", [P, NB + 1], I32)
        unsorted_i = sb("unsorted_flag", [P, 1], I32)

        COLS2 = E2 // P
        records2 = HG[:].rearrange("p b f -> p (b f)")[:, 0:COLS2].bitcast(I32)
        places2 = idx[1][:, 0:COLS2]
        s_half2 = [ctx.enter_context(nc.semaphore(f"scattered2_{h}")) for h in range(2)]
        s_stg2 = ctx.enter_context(nc.semaphore("scatter_staged2"))
        assert COLS2 <= NB * GW and 2 * S2 <= 2 * U * D - 3 * NB * HE

        def scatter_records(pool, rows, flat, records, target, s_stg, s_half, g0, g1):
            def half(g, h):
                nc.gpsimd.tensor_copy(stage[0:rows, h], flat[0:rows, bass.ds(g * (2 * U) + h * U, U)])
                nc.gpsimd.tensor_copy(rec_stage[0:rows, h],
                                      records[0:rows, bass.ds(g * (2 * U) + h * U, U)]).then_inc(s_stg, 1)

            def scatter(h):
                for k in range(U):
                    nc.gpsimd.indirect_dma_start(
                        out=target, out_offset=bass.IndirectOffsetOnAxis(ap=stage[0:rows, h, k:k + 1], axis=0),
                        in_=rec_stage[0:rows, h, k:k + 1], in_offset=None).then_inc(s_half[h], 16)
            for h in range(2):
                half(g0, h)
                pool.wait_ge(s_stg, g0 * 2 + h + 1)
                scatter(h)
            with pool.Fori(g0 + 1, g1) as g:
                for h in range(2):
                    hold(pool, s_half[h], g * (16 * U))
                    half(g, h)
                    hold(pool, s_stg, g * 2 + (h + 1))
                    scatter(h)
            for h in range(2):
                pool.wait_ge(s_half[h], g1 * 16 * U)

        def scatter_second(pool, share):
            done = sum(SHARES[:share])
            scatter_records(pool, P, places2, records2, list_dram[1], s_stg2, s_half2, done, done + SHARES[share])

        BODIES2 = COLS2 // (2 * U)
        SHARES = [BODIES2 * part // 32 for part in (12, 6, 3, 4, 4)]
        SHARES.append(BODIES2 - sum(SHARES))

        def group(i, src_ap, dst_ap, rows, cols, S, first_graph):
            E = rows * cols
            at = [0]

            def area(n, dt=F32):
                a = acc[:, at[0]:at[0] + n]
                at[0] += n
                return a.bitcast(dt) if dt != F32 else a
            if first_graph:
                dst_i, src_i = area(cols, I32), area(cols, I32)
            else:
                dst_i, src_i = places2, records2
            blk_i = area(cols, I32)
            dl_f, pos = area(cols), area(cols)
            cum = [area(cols) for _ in range(2)]
            assert NB < 256
            blk_f, *hot = (a.bitcast(BF16) for a in (area(cols // 2) for _ in range(3)))
            listed, pads = area(S, I32), area(S, I32)
            used = at[0]
            at[0] = 0
            TC = -(-E // P)
            TJ = -(-TC // P)
            raw = [area(TJ * P, I32), area(TJ * P, I32)]
            raw_f = [area(TJ * P), area(TJ * P)]
            src_t, dst_t = area(NB + TJ * P + EXT, I32), area(NB + TJ * P + EXT)
            assert max(at[0], used) <= NB * D
            sm = small[:, 0:2].rearrange("p a b e -> p (a b e)")
            cnt, tot, incl, first, base, q, hits = (sm[:, j * NB:(j + 1) * NB] for j in range(7))
            q_i = q_tab[:, 0:NB]
            bs = sm[:, 7 * NB:7 * NB + S // P]
            bs_i = sm[:, 8 * NB:8 * NB + S // P].bitcast(I32)
            breaks = sm[:, 9 * NB:9 * NB + 1]
            n = f"_{i}"
            HALVES = cols // U
            assert cols % (2 * U) == 0
            hot_bf = onehot[:].rearrange("p a u m -> p (a u m)").bitcast(BF16).rearrange(
                "p (a u m) -> p a u m", a=4, u=U)
            dl_hot = [hot_bf[0:rows, a] for a in range(2)]
            b_hot = [hot_bf[0:rows, 2 + a, :, 0:NB] for a in range(2)]
            (s_in, s_nx, s_brk, s_d, s_hot, s_hotfree, s_deg, s_sq, s_cnt, s_tot, s_bs, s_bsd, s_bsl, s_degc) = (
                sem(c + n) for c in ("edges_in", "next_in", "breaks_counted", "dve_chain", "degree_hots",
                                     "degree_hots_used", "degree_done", "sqrt_done", "counted", "totals",
                                     "step_blocks", "step_blocks_out", "step_blocks_in", "degree_copied"))

            def count_blocks(dve):
                dve.sem_inc(s_cnt, 2)
                with dve.Fori(0, NB // 2) as g:
                    for a in range(2):
                        dve.wait_ge(s_cnt, g * 2 + (a + 1))
                        nc.vector.tensor_scalar(hot[a][0:rows], blk_f[0:rows], iota[0:rows, bass.ds(g * 2 + a, 1)],
                                                0.0, ALU.is_equal, ALU.add,
                                                accum_out=cnt[0:rows, bass.ds(g * 2 + a, 1)]).then_inc(s_cnt, 1)
                dve.wait_ge(s_cnt, NB + 2)

            with nc.Block() as block:
                @block.sync
                def _(sp):
                    sp.dma_start(dst_i[0:rows], dst_ap.rearrange("(p c) -> p c", p=rows)).then_inc(s_in, 16)
                    sp.dma_start(src_i[0:rows], src_ap.rearrange("(p c) -> p c", p=rows)).then_inc(s_in, 16)
                    if first_graph:
                        sp.wait_ge(s_brk, 1)
                        nx = blk_i
                        body = (rows - 1) * cols
                        sp.dma_start(nx[0:rows - 1], dst_ap[1:1 + body].rearrange("(p c) -> p c", p=rows - 1)).then_inc(s_nx, 16)
                        sp.dma_start(nx[rows - 1:rows, 0:cols - 1], dst_ap[1 + body:E].rearrange("(p c) -> p c", p=1)).then_inc(s_nx, 16)
                    sp.wait_ge(s_bs, 1)
                    sp.dma_start(blk_dram[i].rearrange("(j p) -> p j", p=P), bs_i,
                                 allow_slow_non_contiguous=True).then_inc(s_bsd, 16)
                    sp.wait_ge(s_bsd, 16)
                    sp.dma_start(blk[i][:], blk_dram[i].rearrange("(a s) -> a s", a=1)).then_inc(s_bsl, 16)
                    sp.wait_ge(s_bsl, 16)

                @block.vector
                def _(dve):
                    link = Chain(dve, s_d)
                    if first_graph:
                        nc.vector.memset(blk_i[0:rows], N).then_inc(s_brk, 1)
                        dve.wait_ge(s_nx, 32)
                        dve.wait_ge(s_in, 32)
                        link(nc.vector.tensor_tensor(cum[0][0:rows], dst_i[0:rows], blk_i[0:rows], ALU.is_gt))
                        link(nc.vector.tensor_reduce(breaks[0:rows], cum[0][0:rows], AX.X, ALU.add))
                    dve.wait_ge(s_in, 32)
                    link(nc.vector.tensor_scalar(blk_i[0:rows], dst_i[0:rows], 7, None, ALU.logical_shift_right))
                    link(nc.vector.tensor_scalar(dst_i[0:rows], dst_i[0:rows], P - 1, None, ALU.bitwise_and))
                    nc.vector.tensor_copy(blk_f[0:rows], blk_i[0:rows])
                    nc.vector.tensor_copy(dl_f[0:rows], dst_i[0:rows])
                    link(nc.vector.tensor_scalar(dst_i[0:rows], dst_i[0:rows], SRC_BITS, None, ALU.logical_shift_left))
                    link(nc.vector.tensor_tensor(src_i[0:rows], src_i[0:rows], dst_i[0:rows], ALU.bitwise_or))
                    if first_graph:
                        dve.sem_inc(s_hotfree, 2)
                        with dve.Fori(0, HALVES // 2) as g:
                            for a in range(2):
                                dve.wait_ge(s_hotfree, g * 2 + (a + 1))
                                at_c = g * (2 * U) + a * U
                                nc.vector.tensor_tensor(
                                    dl_hot[a], iota[0:rows].unsqueeze(1).broadcast_to([rows, U, P]),
                                    dl_f[0:rows, bass.ds(at_c, U)].unsqueeze(2).broadcast_to([rows, U, P]),
                                    ALU.is_equal)
                                nc.vector.tensor_tensor(
                                    b_hot[a], iota[0:rows, 0:NB].unsqueeze(1).broadcast_to([rows, U, NB]),
                                    blk_f[0:rows, bass.ds(at_c, U)].unsqueeze(2).broadcast_to([rows, U, NB]),
                                    ALU.is_equal).then_inc(s_hot, 1)
                        dve.wait_ge(s_deg, 1)
                        nc.vector.tensor_copy(cnt, ps[:, 1, 0:NB]).then_inc(s_degc, 1)
                    else:
                        count_blocks(dve)
                    dve.wait_ge(s_tot, 1)
                    link(nc.vector.tensor_copy(tot, ps[:, 0, 0:NB]))
                    if first_graph:
                        link(nc.vector.tensor_scalar(breaks, ps[:, 0, NB:NB + 1], 1.0, None, ALU.min))
                        link(nc.vector.tensor_copy(unsorted_i[:], breaks))
                    link(nc.vector.tensor_tensor_scan(incl, tot, tot, 0.0, ALU.add, ALU.max))
                    link(nc.vector.tensor_tensor(first, incl, tot, ALU.subtract))
                    link(nc.vector.tensor_copy(q_i, first))
                    link(nc.vector.tensor_scalar(q_i, q_i, 7, None, ALU.logical_shift_right))
                    link(nc.vector.tensor_copy(q, q_i))
                    link(nc.vector.tensor_tensor(q, q, iota[:, 0:NB], ALU.add))
                    link(nc.vector.tensor_copy(q_i, q))
                    link(nc.vector.memset(q_tab[:, NB:NB + 1], S))
                    for j in range(S // P):
                        link(nc.vector.tensor_scalar(hits, q, step_no[:, j:j + 1], 0.0, ALU.is_le, ALU.add,
                                                     accum_out=bs[:, j:j + 1]))
                    link(nc.vector.tensor_scalar(bs, bs, -1.0, float(D if i == 0 else 1), ALU.add, ALU.mult))
                    nc.vector.tensor_copy(bs_i, bs).then_inc(s_bs, 1)
                    if first_graph:
                        dve.wait_ge(s_sq, 1)
                        link(nc.vector.reciprocal(dinv[:], dinv[:]))

                @block.tensor
                def _(pe):
                    if first_graph:
                        nc.tensor.matmul(ps[:, 1, 0:NB], ident[:], zeros[:, 0:NB], start=True, stop=False)
                        with pe.Fori(0, HALVES // 2) as g:
                            for a in range(2):
                                pe.wait_ge(s_hot, g * 2 + (a + 1))
                                for k in range(U):
                                    mm = nc.tensor.matmul(ps[:, 1, 0:NB], dl_hot[a][:, k], b_hot[a][:, k],
                                                          start=False, stop=False)
                                mm.then_inc(s_hotfree, 1)
                        nc.tensor.matmul(ps[:, 1, 0:NB], ident[:], zeros[:, 0:NB], start=False,
                                         stop=True).then_inc(s_deg, 1)
                        pe.wait_ge(s_degc, 1)
                        nc.tensor.matmul(ps[:, 0, 0:NB], ones[:], cnt, start=True, stop=True)
                        nc.tensor.matmul(ps[:, 0, NB:NB + 1], ones[0:rows], breaks[0:rows], start=True,
                                         stop=True).then_inc(s_tot, 1)
                    else:
                        pe.wait_ge(s_cnt, NB + 2)
                        nc.tensor.matmul(ps[:, 0, 0:NB], ones[0:rows], cnt[0:rows], start=True, stop=True).then_inc(s_tot, 1)

                @block.scalar
                def _(act):
                    if first_graph:
                        act.wait_ge(s_degc, 1)
                        nc.scalar.activation(dinv[:], cnt, ACT.Sqrt, bias=ones[:, 0:1]).then_inc(s_sq, 1)
                if first_graph:
                    @block.gpsimd
                    def _(pool):
                        scatter_second(pool, 0)
            end_phase()

            s_run = sem("running_counts" + n)
            (s_cnt, s_pre, s_d, s_flat, s_padm, s_pad, s_stg, s_tick, s_list) = (
                sem(c + n) for c in ("counted", "prefix_done", "dve_chain", "places_done", "pads_made", "pads_stored",
                                     "scatter_staged", "pool_tick", "list_in"))
            s_half = [sem(f"scattered{h}" + n) for h in range(2)]
            flat = dst_i

            def general(eng, run):
                if not first_graph:
                    return run()
                flag = eng.value_load(unsorted_i[0:1, 0:1], min_val=0, max_val=1)
                with eng.If(flag > 0):
                    run()

            with nc.Block() as block:
                @block.sync
                def _(sp):
                    def run():
                        sp.wait_ge(s_padm, 1)
                        sp.dma_start(list_dram[i].rearrange("(p s) a -> p (s a)", p=P), pads).then_inc(s_pad, 16)
                        if not first_graph:
                            sp.wait_ge(s_pad, 16)
                            return
                        for h in range(2):
                            sp.wait_ge(s_half[h], 16 * U * (HALVES // 2))
                        sp.dma_start(listed, list_dram[i].rearrange("(p s) a -> p (s a)", p=P)).then_inc(s_list, 16)
                    general(sp, run)

                @block.vector
                def _(dve):
                    def run():
                        link = Chain(dve, s_d)
                        nc.vector.memset(pads, NO_DST << SRC_BITS).then_inc(s_padm, 1)
                        if first_graph:
                            count_blocks(dve)
                        dve.wait_ge(s_pre, 1)
                        link(nc.vector.scalar_tensor_tensor(base, ps[:, 0, NB:2 * NB], -1.0, first, ALU.add, ALU.add))
                        link(nc.vector.memset(pos[0:rows], 0.0))
                        with dve.Fori(0, NB // 2) as g:
                            for a in range(2):
                                nc.vector.tensor_scalar(hot[a][0:rows], blk_f[0:rows],
                                                        iota[0:rows, bass.ds(g * 2 + a, 1)], None,
                                                        ALU.is_equal).then_inc(s_run, 1)
                            for a in range(2):
                                dve.wait_ge(s_run, a + 1)
                                nc.vector.tensor_tensor_scan(cum[a][0:rows], hot[a][0:rows], hot[a][0:rows],
                                                             base[0:rows, bass.ds(g * 2 + a, 1)],
                                                             ALU.add, ALU.bypass).then_inc(s_run, 1)
                            for a in range(2):
                                dve.wait_ge(s_run, a * 2 + 3)
                                nc.vector.copy_predicated(pos[0:rows], hot[a][0:rows].bitcast(mybir.dt.uint16),
                                                          cum[a][0:rows]).then_inc(s_run, 1)
                            dve.wait_ge(s_run, 6)
                            dve.sem_clear(s_run)
                        link(nc.vector.tensor_copy(dst_i[0:rows], pos[0:rows]))
                        link(nc.vector.tensor_scalar(blk_i[0:rows], dst_i[0:rows], 7, None, ALU.logical_shift_right))
                        link(nc.vector.tensor_scalar(dst_i[0:rows], dst_i[0:rows], P - 1, None, ALU.bitwise_and))
                        nc.vector.tensor_copy(cum[0][0:rows], blk_i[0:rows])
                        link(nc.vector.tensor_copy(pos[0:rows], dst_i[0:rows]))
                        link(nc.vector.tensor_tensor(cum[0][0:rows], cum[0][0:rows], blk_f[0:rows], ALU.add))
                        link(nc.vector.scalar_tensor_tensor(pos[0:rows], pos[0:rows], float(S), cum[0][0:rows],
                                                            ALU.mult, ALU.add))
                        nc.vector.tensor_copy(flat[0:rows], pos[0:rows]).then_inc(s_flat, 1)
                        if not first_graph:
                            return
                        dve.wait_ge(s_list, 16)
                        nc.vector.tensor_scalar(idx[i][:, 0:S], listed, (1 << SRC_BITS) - 1, None, ALU.bitwise_and)
                        link(nc.vector.tensor_scalar(pads, listed, SRC_BITS, None, ALU.logical_shift_right))
                        link(nc.vector.tensor_copy(dloc[i][:, 0:S], pads))
                    general(dve, run)

                @block.tensor
                def _(pe):
                    def run():
                        if first_graph:
                            pe.wait_ge(s_cnt, NB + 2)
                        nc.tensor.matmul(ps[:, 0, NB:2 * NB], lower[0:rows], cnt[0:rows], start=True,
                                         stop=True).then_inc(s_pre, 1)
                    general(pe, run)

                if first_graph:
                    @block.gpsimd
                    def _(pool):
                        def run():
                            pool.wait_ge(s_flat, 1)
                            pool.wait_ge(s_pad, 16)
                            scatter_records(pool, rows, flat, src_i, list_dram[i], s_stg, s_half, 0, HALVES // 2)
                        general(pool, run)
            end_phase()
            if not first_graph:
                return

            s_laid, s_m, s_r, s_f, s_tp, s_tc = (sem(c) for c in ("laid_out", "raw_cleared", "raw_in", "raw_floats", "turned", "turned_copied"))
            full = TC // P * P
            rest = E // P - full
            tail = E - (full + rest) * P
            assert tail > 0 and TJ * P <= 4 * 512

            def sorted_case(eng, run):
                flag = eng.value_load(unsorted_i[0:1, 0:1], min_val=0, max_val=1)
                with eng.If(flag < 1):
                    run()

            with nc.Block() as block:
                @block.sync
                def _(sp):
                    def run():
                        sp.wait_ge(s_m, 1)
                        for a, v in enumerate((src_ap, dst_ap)):
                            sp.dma_start(raw[a][:, 0:full].rearrange("t (j p) -> t j p", p=P),
                                         v[0:full * P].rearrange("(j t p) -> t j p", t=P, p=P)).then_inc(s_r, 16)
                            sp.dma_start(raw[a][0:rest, full:full + P],
                                         v[full * P:(full + rest) * P].rearrange("(t p) -> t p", p=P)).then_inc(s_r, 16)
                            sp.dma_start(raw[a][rest:rest + 1, full:full + tail],
                                         v[(full + rest) * P:E].rearrange("(t p) -> t p", t=1)).then_inc(s_r, 16)
                    sorted_case(sp, run)

                @block.vector
                def _(dve):
                    def run():
                        nc.vector.memset(raw[0][:, full:full + P], 0)
                        nc.vector.memset(raw[1][:, full:full + P], 1 << 20).then_inc(s_m, 1)
                        dve.wait_ge(s_r, 96)
                        nc.vector.tensor_copy(raw_f[0], raw[0])
                        nc.vector.tensor_copy(raw_f[1], raw[1]).then_inc(s_f, 1)
                        dve.wait_ge(s_tp, 1)
                        nc.vector.tensor_copy(src_t[:, NB:NB + TJ * P], ps[:, 0:4].rearrange("p a f -> p (a f)")[:, 0:TJ * P])
                        nc.vector.tensor_copy(dst_t[:, NB:NB + TJ * P],
                                              ps[:, 4:8].rearrange("p a f -> p (a f)")[:, 0:TJ * P]).then_inc(s_tc, 1)
                        dve.wait_ge(s_tc, 1)
                        with dve.Fori(0, NB) as b:
                            _, (q0, q1) = nc.values_load_multi_w_load_instructions(
                                q_tab[0:1, bass.ds(b, 2)], engines=[mybir.EngineType.DVE], min_val=0, max_val=S,
                                skip_runtime_bounds_check_because="first steps of blocks, counted on the chip")
                            with dve.Fori(q0, q1, EXT) as s:
                                tile = s - b + NB
                                nc.vector.tensor_copy(idx[0][:, bass.ds(s, EXT)], src_t[:, bass.ds(tile, EXT)]).then_inc(s_laid, 1)
                                nc.vector.tensor_scalar(dloc[0][:, bass.ds(s, EXT)], dst_t[:, bass.ds(tile, EXT)],
                                                        node0[:, bass.ds(b, 1)], None, ALU.subtract).then_inc(s_laid, 1)
                                dve.wait_ge(s_laid, 2)
                                dve.sem_clear(s_laid)
                    sorted_case(dve, run)

                @block.tensor
                def _(pe):
                    def run():
                        pe.wait_ge(s_f, 1)
                        for a in range(2):
                            for j in range(TJ):
                                mm = nc.tensor.transpose(ps[:, 4 * a + j // 4, (j % 4) * P:(j % 4 + 1) * P],
                                                         raw_f[a][:, j * P:(j + 1) * P], ident[:])
                        mm.then_inc(s_tp, 1)
                    sorted_case(pe, run)

                @block.gpsimd
                def _(pool):
                    scatter_second(pool, 1)
            end_phase()

        rows1 = 125
        group(1, edges2[0], edges2[1], P, COLS2, S2, False)
        group(0, src, dst, rows1, E1 // rows1, S1, True)

        CHUNKS = 7
        PER = NB // CHUNKS
        assert PER * CHUNKS == NB
        s_xc = [sem(f"x_in_chunk{c}") for c in range(CHUNKS)]
        s_xm, s_t0, s_tw = sem("x_tail_cleared"), sem("t0_done"), sem("t0_out")
        s_n, s_sqr = sem("norm_chain"), sem("std_done")

        def moments(link, ready):
            link(nc.vector.tensor_tensor(mv[:, :, 0], stats[:, :, 1], stats[:, :, 4], ALU.add))
            link(nc.vector.tensor_tensor(mv[:, :, 1], stats[:, :, 1], stats[:, :, 4], ALU.subtract))
            link(nc.vector.tensor_scalar(mv[:, :, 0], mv[:, :, 0], 0.5, None, ALU.mult))
            link(nc.vector.scalar_tensor_tensor(mv[:, :, 1], mv[:, :, 1], 0.25, mv[:, :, 1], ALU.mult, ALU.mult))
            link(nc.vector.tensor_tensor(stats[:, :, 0], stats[:, :, 2], stats[:, :, 5], ALU.add))
            link(nc.vector.scalar_tensor_tensor(mv[:, :, 1], stats[:, :, 0], 1.0 / D, mv[:, :, 1],
                                                ALU.mult, ALU.add))
            link.eng.sem_inc(ready, 1)

        with nc.Block() as block:
            s_st, s_ag = sem("stats0"), sem("stats0_all")

            @block.sync
            def _(sp):
                sp.wait_ge(s_xm, 1)
                for c in range(CHUNKS):
                    b0, b1 = c * PER, min((c + 1) * PER, NB - 1)
                    sp.dma_start(acc[:, b0 * D:b1 * D].rearrange("p (b f) -> p b f", f=D),
                                 x[b0 * P:b1 * P].rearrange("(b p) f -> p b f", p=P)).then_inc(s_xc[c], 16)
                sp.dma_start(acc[0:TAIL, (NB - 1) * D:NB * D], x[(NB - 1) * P:N]).then_inc(s_xc[CHUNKS - 1], 16)
                for c in range(CHUNKS):
                    sp.wait_ge(s_t0, (c + 1) * PER)
                    at = slice(c * PER * P, (c + 1) * PER * P)
                    sp.dma_start(table[at].rearrange("(b p) f -> p b f", p=P),
                                 acc[:, c * PER * D:(c + 1) * PER * D].rearrange("p (b f) -> p b f", f=D)).then_inc(s_tw, 16)
                sp.wait_ge(s_tw, 16 * CHUNKS)

            @block.vector
            def _(dve):
                link = Chain(dve, s_n)
                nc.vector.memset(acc[:, (NB - 1) * D:NB * D], 0.0).then_inc(s_xm, 1)
                for c in range(CHUNKS):
                    dve.wait_ge(s_xc[c], 32 if c == CHUNKS - 1 else 16)
                    with dve.Fori(c * PER, (c + 1) * PER) as b:
                        nc.vector.bn_stats(stats[:, bass.ds(b, 1)].rearrange("p a s -> p (a s)"),
                                           acc[:, bass.ds(b * D, D)]).then_inc(s_st, 1)
                dve.wait_ge(s_st, NB)
                moments(link, s_ag)
                dve.wait_ge(s_sqr, 1)
                link(nc.vector.reciprocal(rstd[:], rstd[:]))
                link(nc.vector.tensor_tensor(rstd[:], rstd[:], dinv[:], ALU.mult))
                with dve.Fori(0, NB) as b:
                    nc.vector.tensor_scalar(acc[:, bass.ds(b * D, D)], acc[:, bass.ds(b * D, D)],
                                            mv[:, bass.ds(b, 1), 0], rstd[:, bass.ds(b, 1)],
                                            ALU.subtract, ALU.mult).then_inc(s_t0, 1)

            @block.scalar
            def _(act):
                act.wait_ge(s_ag, 1)
                nc.scalar.activation(rstd[:], mv[:, :, 1], ACT.Sqrt, bias=eps[:, 0:1]).then_inc(s_sqr, 1)

            @block.gpsimd
            def _(pool):
                scatter_second(pool, 2)

        end_phase()

        ring = work[:].rearrange("p (h u f) -> p h u f", h=2, u=U)
        G1 = S1 // (2 * U)
        Q = 4

        def aggregate(l):
            n = f"_l{l}"
            s_row = [sem(f"rows_in{h}" + n) for h in range(2)]
            s_stg, s_tick = sem("indices_staged" + n), sem("pool_tick" + n)
            s_used = sem("ring_half_used" + n)
            s_hot, s_mm, s_add, s_sum = sem("onehots" + n), sem("products" + n), sem("adds" + n), sem("psum_free" + n)
            with nc.Block() as block:
                @block.gpsimd
                def _(pool):
                    with pool.Fori(0, G1) as g:
                        for h in range(2):
                            pool.wait_ge(s_used, g * 2 + (h + 1))
                            pool.sem_inc(s_tick, 1)
                            nc.gpsimd.tensor_copy(stage[:, h], idx[0][:, bass.ds(g * (2 * U) + h * U, U)]).then_inc(s_stg, 1)
                            pool.wait_ge(s_stg, g * 2 + (h + 1))
                            pool.sem_inc(s_tick, 1)
                            for k in range(U):
                                nc.gpsimd.indirect_dma_start(
                                    out=ring[:, h, k], out_offset=None, in_=table,
                                    in_offset=bass.IndirectOffsetOnAxis(ap=stage[:, h, k:k + 1], axis=0),
                                ).then_inc(s_row[h], 16)

                @block.tensor
                def _(pe):
                    pe.sem_inc(s_used, 2)
                    with pe.Fori(0, G1) as g:
                        for h in range(2):
                            pe.wait_ge(s_row[h], (g + 1) * (16 * U))
                            pe.wait_ge(s_hot, g * 2 + (h + 1))
                            for k in range(U):
                                bank = (k // 2) % 8
                                if k % Q == 0:
                                    pe.wait_ge(s_sum, g * (2 * U // Q) + (h * U + k) // Q + 1)
                                mm = nc.tensor.matmul(ps[:, bank, (k % 2) * D:(k % 2 + 1) * D], onehot[:, h, k],
                                                      ring[:, h, k], start=True, stop=True, skip_group_check=True)
                                if k % Q == Q - 1:
                                    mm.then_inc(s_mm, 1)
                            pe.wait_ge(s_mm, g * (2 * U // Q) + (h + 1) * (U // Q))
                            pe.sem_inc(s_used, 1)

                @block.vector
                def _(dve):
                    dve.sem_inc(s_sum, U // Q)
                    def hots(g, h):
                        nc.vector.tensor_tensor(
                            onehot[:, h], iota[:].unsqueeze(1).broadcast_to([P, U, P]),
                            dloc[0][:, bass.ds(g * (2 * U) + h * U, U)].unsqueeze(2).broadcast_to([P, U, P]),
                            ALU.is_equal).then_inc(s_hot, 1)
                    with dve.Fori(0, G1) as g:
                        for h in range(2):
                            dve.wait_ge(s_used, g * 2 + (h + 1))
                            hots(g, h)
                            for k in range(U):
                                bank = (k // 2) % 8
                                if k % 8 == 0:
                                    base = load_blocks(mybir.EngineType.DVE, 0, g * (2 * U) + (h * U + k), top=(NB - 1) * D)
                                if k % Q == 0:
                                    dve.wait_ge(s_mm, g * (2 * U // Q) + (h * U + k) // Q + 1)
                                at = bass.ds(base[k % 8], D)
                                nc.vector.tensor_tensor(acc[:, at], acc[:, at], ps[:, bank, (k % 2) * D:(k % 2 + 1) * D],
                                                        ALU.add).then_inc(s_add, 1)
                                dve.wait_ge(s_add, h * U + k + 1)
                                if k % Q == Q - 1:
                                    dve.sem_inc(s_sum, 1)
                        dve.sem_clear(s_add)

        zst, zt, ust, xin = (work[:, j * 4 * D:(j + 1) * 4 * D].rearrange("p (r a f) -> p r a f", r=2, a=2)
                             for j in range(4))
        flat2 = lambda v: v.rearrange("p a f -> p (a f)")

        def turn_pair(n, r, s_from, s_free, s_to):
            nc.tensor.wait_ge(s_from, n + 1)
            nc.tensor.wait_ge(s_free, n + 1)
            for a in range(2):
                for k in range(KD):
                    mm = nc.tensor.transpose(ps[:, r, (a * KD + k) * P:(a * KD + k + 1) * P],
                                             zst[:, r, a, k * P:(k + 1) * P], ident[:])
            mm.then_inc(s_to, 1)

        def finish(l):
            last = l == 2
            n_ = f"_f{l}"
            s_z, s_zp, s_zt, s_y, s_v, s_u, s_a, s_o = (sem(c + n_) for c in (
                "scaled", "transposed", "transposed_copied", "weighted", "biased", "activated", "pair_done", "pair_out"))
            s_xi = [sem(f"x_in{r}" + n_) for r in range(2)]
            s_xt = sem("x_tail_in" + n_)
            with nc.Block() as block:
                @block.gpsimd
                def _(pool):
                    scatter_second(pool, 3 + l)

                @block.scalar
                def _(act):
                    act.sem_inc(s_u, 2)

                    def scale(n, r):
                        act.wait_ge(s_zp, n + 1)
                        for a in range(2):
                            b = n * 2 + a
                            ins = nc.scalar.activation(zst[:, r, a], acc[:, bass.ds(b * D, D)], ACT.Copy,
                                                       scale=dinv[:, bass.ds(b, 1)])
                        ins.then_inc(s_z, 1)

                    def activate(n, r):
                        act.wait_ge(s_v, n + 3)
                        if last:
                            act.sem_inc(s_u, 1)
                        else:
                            nc.scalar.activation(flat2(ust[:, r]), flat2(ust[:, r]), ACT.Gelu_apprx_tanh).then_inc(s_u, 1)
                    skewed(act, PAIRS, (0, scale), (3, activate))

                @block.tensor
                def _(pe):
                    pe.sem_inc(s_zp, 2)
                    pe.sem_inc(s_y, 2)

                    def weigh(n, r):
                        pe.wait_ge(s_zt, n + 3)
                        pe.wait_ge(s_v, n + 1)
                        for a in range(2):
                            for k in range(KD):
                                mm = nc.tensor.matmul(ps[:, 2 + r, a * D:(a + 1) * D], zt[:, r, a, k * P:(k + 1) * P],
                                                      gw_sb[:, l, k], start=(k == 0), stop=(k == KD - 1),
                                                      skip_group_check=True)
                        mm.then_inc(s_y, 1)
                    skewed(pe, PAIRS, (2, weigh), (0, lambda n, r: turn_pair(n, r, s_z, s_zt, s_zp)))

                @block.vector
                def _(dve):
                    dve.sem_inc(s_zt, 2)
                    dve.sem_inc(s_v, 2)
                    dve.sem_inc(s_a, 2)

                    def turned(n, r):
                        dve.wait_ge(s_zp, n + 3)
                        dve.wait_ge(s_y, n + 1)
                        nc.vector.tensor_copy(flat2(zt[:, r]), ps[:, r]).then_inc(s_zt, 1)

                    def bias(n, r):
                        dve.wait_ge(s_y, n + 3)
                        dve.wait_ge(s_a, n + 1)
                        nc.vector.tensor_tensor(ust[:, r], ps[:, 2 + r].rearrange("p (a f) -> p a f", a=2),
                                                gb_sb[:, l].unsqueeze(1).broadcast_to([P, 2, D]), ALU.add).then_inc(s_v, 1)

                    def keep(n, r):
                        dve.wait_ge(s_u, n + 3)
                        if last:
                            dve.wait_ge(s_xi[r], pair_use(n, r))
                            if isinstance(n, int) and n == PAIRS - 1:
                                dve.wait_ge(s_xt, 16)
                        for a in range(2):
                            b = n * 2 + a
                            if not last:
                                ins = nc.vector.tensor_scalar(acc[:, bass.ds(b * D, D)], ust[:, r, a], dinv[:, bass.ds(b, 1)],
                                                              None, ALU.mult)
                            else:
                                ins = nc.vector.tensor_tensor(acc[:, bass.ds(b * D, D)], ust[:, r, a], xin[:, r, a], ALU.add)
                        ins.then_inc(s_a, 1)

                    def pair_use(n, r):
                        return n * 8 + (16 - 8 * r)

                    def moments_of(n, r):
                        dve.wait_ge(s_a, n + 3)
                        for a in range(2):
                            b = n * 2 + a
                            nc.vector.bn_stats(stats[:, bass.ds(b, 1)].rearrange("p a s -> p (a s)"),
                                               acc[:, bass.ds(b * D, D)])
                    skewed(dve, PAIRS, (0, turned), (2, bias), (3, keep), *([(4, moments_of)] if last else []))

                @block.sync
                def _(sp):
                    dest = x1_dram if last else table

                    def load(n, r):
                        sp.dma_start(xin[:, r], x[bass.ds(n * 2 * P, 2 * P)].rearrange("(a p) f -> p a f", p=P)).then_inc(s_xi[r], 16)

                    def store(n, r, more):
                        hold(sp, s_a, n + 3)
                        sp.dma_start(dest[bass.ds(n * 2 * P, 2 * P)].rearrange("(a p) f -> p a f", p=P),
                                     acc[:, bass.ds(n * 2 * D, 2 * D)].rearrange("p (a f) -> p a f", a=2)).then_inc(s_o, 16)
                        if last and more:
                            load(n + 2, r)
                    if last:
                        load(0, 0)
                        load(1, 1)
                    with sp.Fori(0, (PAIRS - 3) // 2) as g:
                        for r in range(2):
                            store(g * 2 + r, r, True)
                    store(PAIRS - 3, 0, False)
                    if last:
                        f = (PAIRS - 1) * 2 * P
                        sp.dma_start(xin[:, 0, 0], x[f:f + P]).then_inc(s_xi[0], 16)
                        sp.dma_start(xin[0:TAIL, 0, 1], x[f + P:N]).then_inc(s_xt, 16)
                    store(PAIRS - 2, 1, False)
                    store(PAIRS - 1, 0, False)
                    sp.wait_ge(s_o, 16 * PAIRS)

        for l in range(3):
            aggregate(l)
            finish(l)
            end_phase()

        s_l2, s_u2 = sem("list2_in"), sem("list2_unpack")
        listed2, locals2 = (work[:, j * S2:(j + 1) * S2].bitcast(I32) for j in range(2))
        with nc.Block() as block:
            @block.sync
            def _(sp):
                sp.dma_start(listed2, list_dram[1].rearrange("(p s) a -> p (s a)", p=P)).then_inc(s_l2, 16)

            @block.vector
            def _(dve):
                link = Chain(dve, s_u2)
                dve.wait_ge(s_l2, 16)
                nc.vector.tensor_scalar(idx[1][:], listed2, (1 << SRC_BITS) - 1, None, ALU.bitwise_and)
                link(nc.vector.tensor_scalar(locals2, listed2, SRC_BITS, None, ALU.logical_shift_right))
                nc.vector.memset(dloc[1][:, S2:S2 + U], NO_DST)
                link(nc.vector.tensor_copy(dloc[1][:, 0:S2], locals2))
        end_phase()

        s_ag, s_sqr, s_n = sem("stats1_all"), sem("std1_done"), sem("chain1")
        s_xn, s_xp, s_xt, s_h, s_hc = (sem(c) for c in (
            "xn", "xn_transposed", "xn_t_copied", "h_done", "h_copied"))
        s_xo = [sem(f"xn_t_out{r}") for r in range(2)]
        s_g, s_go = sem("gat_rows"), sem("gat_table_out")
        h16 = HG[:, :, 0:HE]
        with nc.Block() as block:
            @block.vector
            def _(dve):
                link = Chain(dve, s_n)
                moments(link, s_ag)
                dve.wait_ge(s_sqr, 1)
                link(nc.vector.reciprocal(rstd[:], rstd[:]))
                dve.sem_inc(s_hc, 2)

                def norm(n, r):
                    dve.wait_ge(s_xp, n + 1)
                    for a in range(2):
                        b = n * 2 + a
                        ins = nc.vector.tensor_scalar(zst[:, r, a], acc[:, bass.ds(b * D, D)],
                                                      mv[:, bass.ds(b, 1), 0], rstd[:, bass.ds(b, 1)],
                                                      ALU.subtract, ALU.mult)
                    ins.then_inc(s_xn, 1)

                def keep_h(n, r):
                    dve.wait_ge(s_h, n + 3)
                    nc.vector.tensor_copy(HG[:, bass.ds(n * 2, 2), 0:HE],
                                          ps[:, 2 + r, 0:2 * HE].rearrange("p (a e) -> p a e", a=2)).then_inc(s_hc, 1)
                skewed(dve, PAIRS, (0, norm), (3, keep_h))
                dve.wait_ge(s_hc, PAIRS + 2)
                for which, to in ((0, HG[:, :, HE:GW]), (1, ad[:])):
                    link(nc.vector.tensor_tensor(small[:, which], h16, row16[:, which].unsqueeze(1).broadcast_to([P, NB, HE]),
                                                 ALU.mult))
                    link(nc.vector.tensor_reduce(to, small[:, which].rearrange("p b (h e) -> p b h e", e=NE), AX.X, ALU.add))
                nc.vector.tensor_copy(emx[:], HG[:, :, HE:GW]).then_inc(s_g, 1)

            @block.scalar
            def _(act):
                act.wait_ge(s_ag, 1)
                nc.scalar.activation(rstd[:], mv[:, :, 1], ACT.Sqrt, bias=eps[:, 0:1]).then_inc(s_sqr, 1)
                act.sem_inc(s_xt, 2)

                def turned(n, r):
                    act.wait_ge(s_xp, n + 3)
                    act.wait_ge(s_h, n + 1)
                    act.wait_ge(s_xo[r], n * 8 + (16 - 8 * r))
                    nc.scalar.copy(flat2(zt[:, r]), ps[:, r]).then_inc(s_xt, 1)
                skewed(act, PAIRS, (0, turned))

            @block.tensor
            def _(pe):
                pe.sem_inc(s_xp, 2)
                pe.sem_inc(s_h, 2)

                def heads(n, r):
                    pe.wait_ge(s_xt, n + 3)
                    pe.wait_ge(s_hc, n + 1)
                    for a in range(2):
                        for k in range(KD):
                            mm = nc.tensor.matmul(ps[:, 2 + r, a * HE:(a + 1) * HE], zt[:, r, a, k * P:(k + 1) * P],
                                                  wg_sb[:, k], start=(k == 0), stop=(k == KD - 1), skip_group_check=True)
                    mm.then_inc(s_h, 1)
                skewed(pe, PAIRS, (2, heads), (0, lambda n, r: turn_pair(n, r, s_xn, s_xt, s_xp)))

            @block.sync
            def _(sp):
                for r in range(2):
                    sp.sem_inc(s_xo[r], 16)

                def store(n, r):
                    hold(sp, s_xt, n + 3)
                    sp.dma_start(xnt_dram[bass.ds(n * 2, 2)].rearrange("a p f -> p a f"), zt[:, r]).then_inc(s_xo[r], 16)
                skewed(sp, PAIRS, (0, store))
                for r in range(2):
                    sp.wait_ge(s_xo[r], 16 * ((PAIRS + 1 - r) // 2 + 1))
                sp.wait_ge(s_g, 1)
                sp.dma_start(gat_table.rearrange("(b p) f -> p b f", p=P), HG[:]).then_inc(s_go, 16)
                sp.wait_ge(s_go, 16)

        end_phase()

        G2 = S2 // (2 * U)
        grow = work[:, 0:2 * U * GW].rearrange("p (h u f) -> p h u f", h=2, u=U)
        penal = work[:, 1024:1024 + U * P].bitcast(BF16).rearrange("p (h u m) -> p h u m", h=2, u=U)
        pairs4 = onehot[:].rearrange("p h u m -> p (h u m)")[:, 0:4 * NH * P].rearrange("p (a j m) -> p a j m", a=4, j=NH)
        s_pair = sem("pairs_made")
        mx = work[:, 4096:4096 + 2 * U * NH].rearrange("p (h u k) -> p h u k", h=2, u=U)
        rows_kept = acc[:, 0:S2 * GW]
        s_row = [sem(f"gat_rows_in{h}") for h in range(2)]
        s_stg, s_tick, s_used = sem("gat_staged"), sem("gat_tick"), sem("gat_half_used")
        s_hot, s_mm, s_mrg, s_keep = sem("gat_penalties"), sem("gat_scores"), sem("gat_merged"), sem("gat_rows_kept")
        s_pf = sem("gat_psum_free")
        with nc.Block() as block:
            @block.gpsimd
            def _(pool):
                with pool.Fori(0, G2) as g:
                    for h in range(2):
                        pool.wait_ge(s_used, g * 2 + (h + 1))
                        pool.sem_inc(s_tick, 1)
                        pool.wait_ge(s_keep, g * 2 + (h + 1))
                        pool.sem_inc(s_tick, 1)
                        nc.gpsimd.tensor_copy(stage[:, h], idx[1][:, bass.ds(g * (2 * U) + h * U, U)]).then_inc(s_stg, 1)
                        pool.wait_ge(s_stg, g * 2 + (h + 1))
                        pool.sem_inc(s_tick, 1)
                        for k in range(U):
                            nc.gpsimd.indirect_dma_start(
                                out=grow[:, h, k], out_offset=None, in_=gat_table,
                                in_offset=bass.IndirectOffsetOnAxis(ap=stage[:, h, k:k + 1], axis=0),
                            ).then_inc(s_row[h], 16)

            @block.scalar
            def _(act):
                act.sem_inc(s_keep, 2)
                with act.Fori(0, G2) as g:
                    for h in range(2):
                        act.wait_ge(s_row[h], (g + 1) * (16 * U))
                        nc.scalar.copy(rows_kept[:, bass.ds((g * (2 * U) + h * U) * GW, U * GW)],
                                       grow[:, h].rearrange("p u f -> p (u f)")).then_inc(s_keep, 1)
                        act.wait_ge(s_hot, g * 2 + (h + 1))
                        for k in range(U):
                            act.wait_ge(s_mm, g * (2 * U) + (h * U + k + 1))
                            for j in range(NH):
                                ins = nc.scalar.activation(pairs4[:, k % 4, j], penal[:, h, k], ACT.Identity,
                                                           bias=grow[:, h, k, HE + j:HE + j + 1], scale=BIG)
                            ins.then_inc(s_pair, 1)

            @block.tensor
            def _(pe):
                pe.sem_inc(s_used, 2)
                pe.sem_inc(s_mm, 4)
                with pe.Fori(0, G2) as g:
                    for h in range(2):
                        for k in range(U):
                            pe.wait_ge(s_pf, g * (2 * U) + (h * U + k + 1))
                            bank = k % 8
                            pe.wait_ge(s_pair, g * (2 * U) + (h * U + k + 1))
                            for j in range(NH):
                                mm = nc.tensor.transpose(ps[:, bank, j * P:(j + 1) * P], pairs4[:, k % 4, j], ident[:])
                            mm.then_inc(s_mm, 1)
                        pe.wait_ge(s_mm, g * (2 * U) + ((h + 1) * U + 4))
                        pe.sem_inc(s_used, 1)

            @block.vector
            def _(dve):
                def penalties(h, columns):
                    nc.vector.tensor_tensor(
                        penal[:, h], iota[:].unsqueeze(1).broadcast_to([P, U, P]),
                        dloc[1][:, columns].unsqueeze(2).broadcast_to([P, U, P]), ALU.not_equal).then_inc(s_hot, 1)

                penalties(0, slice(0, U))
                dve.sem_inc(s_pf, 8)
                with dve.Fori(0, G2) as g:
                    for h in range(2):
                        for k in range(U):
                            if k == U // 2:
                                dve.wait_ge(s_used, g * 2 + (h + 2))
                                penalties(1 - h, bass.ds(g * (2 * U) + (h + 1) * U, U))
                            dve.wait_ge(s_mm, g * (2 * U) + (h * U + k + 5))
                            nc.vector.tensor_reduce(mx[:, h, k], ps[:, k % 8].rearrange("p (j e) -> p j e", j=NH),
                                                    AX.X, ALU.max).then_inc(s_pf, 1)
                            if k % 8 == 7:
                                dve.wait_ge(s_pf, g * (2 * U) + (h * U + k + 9))
                                block_at = load_blocks(mybir.EngineType.DVE, 1, g * (2 * U) + (h * U + k - 7))
                                for j in range(8):
                                    to = emx[:, bass.ds(block_at[j], 1)].rearrange("p a k -> p (a k)")
                                    nc.vector.tensor_tensor(to, to, mx[:, h, k - 7 + j], ALU.max).then_inc(s_mrg, 1)
                                    dve.wait_ge(s_mrg, h * U + k - 7 + j + 1)
                    dve.sem_clear(s_mrg)

        end_phase()

        s_e, s_ee, s_eo = sem("self_scores"), sem("self_exp"), sem("self_chain")
        sc = small[:, 2, :, 0:NH]
        sc2 = small[:, 2, :, NH:2 * NH]
        with nc.Block() as block:
            @block.vector
            def _(dve):
                link = Chain(dve, s_eo)
                link(nc.vector.tensor_tensor(sc, emx[:], ad[:], ALU.add))
                link(nc.vector.scalar_tensor_tensor(V[:, :, NH:2 * NH], sc, 0.2, sc, ALU.mult, ALU.max))
                link(nc.vector.tensor_copy(V[:, :, 0:NH], ad[:]))
                link(nc.vector.tensor_tensor(sc, HG[:, :, HE:GW], ad[:], ALU.add))
                link(nc.vector.scalar_tensor_tensor(sc2, sc, 0.2, sc, ALU.mult, ALU.max))
                link(nc.vector.tensor_tensor(sc, sc2, V[:, :, NH:2 * NH], ALU.subtract))
                dve.sem_inc(s_e, 1)
                left = work[:, 1024:1024 + NB * 2 * NH].rearrange("p (b f) -> p b f", f=2 * NH)
                link(nc.vector.tensor_copy(V3[:, :, :, 0], V[:]))
                link(nc.vector.tensor_tensor(left, V[:], V3[:, :, :, 0], ALU.subtract))
                link(nc.vector.tensor_copy(V3[:, :, :, 1], left))
                link(nc.vector.tensor_tensor(left, left, V3[:, :, :, 1], ALU.subtract))
                link(nc.vector.tensor_copy(V3[:, :, :, 2], left))
                dve.wait_ge(s_ee, 1)
                link(nc.vector.tensor_copy(AGG[:, :, HE:GW], sc2))
                for j in range(NH):
                    link(nc.vector.tensor_tensor(AGG[:, :, j * NE:(j + 1) * NE], HG[:, :, j * NE:(j + 1) * NE],
                                                 sc2[:, :, j:j + 1].broadcast_to([P, NB, NE]), ALU.mult))

            @block.scalar
            def _(act):
                act.wait_ge(s_e, 1)
                nc.scalar.activation(sc2, sc, ACT.Exp).then_inc(s_ee, 1)

        end_phase()

        oht = work[:, 0:U * P // 2].bitcast(BF16).rearrange("p (u m) -> p u m", u=U)
        msg = work[:, U * P:U * P + 2 * U * GW].rearrange("p (h u f) -> p h u f", h=2, u=U)
        sc3 = work[:, 4096:4096 + 3 * U * NH].rearrange("p (a u k) -> p a u k", a=3, u=U)
        kept = rows_kept.rearrange("p (s f) -> p s f", f=GW)
        (s_mm3, s_hot, s_tp, s_tc, s_dist, s_sc, s_ex, s_msg, s_mm, s_add, s_c3, s_loc) = (sem("b2_" + c) for c in (
            "onehots_used",
            "onehots", "transposed", "transposed_copied", "distributed", "scores", "exps", "messages", "products", "adds",
            "chain", "half_adds"))
        s_vst = sem("b2_node_values_staged")
        vst = work[:, 4288:4288 + 2 * U * 3 * NH].bitcast(BF16).rearrange("p (h u f) -> p h u f", h=2, u=U)
        edge_v = work[:, 4672:4672 + U * 2 * NH].rearrange("p (u f) -> p u f", u=U)
        halves = 2 * G2
        hot3 = [onehot[:, 0], onehot[:, 1], work[:, 6144:6144 + U * P].rearrange("p (u m) -> p u m", u=U)]
        assert halves % 6 == 0
        d8 = [ps[:, 4 + r, 0:U * 6 * NH].rearrange("p (u f c) -> p u f c", u=U, c=3) for r in range(2)]
        with nc.Block() as block:
            @block.vector
            def _(dve):
                dve.sem_inc(s_add, 2)

                def hots(n, r):
                    dve.wait_ge(s_mm3, n + 1)
                    nc.vector.tensor_tensor(
                        hot3[r % 3], iota[:].unsqueeze(1).broadcast_to([P, U, P]),
                        dloc[1][:, bass.ds(n * U, U)].unsqueeze(2).broadcast_to([P, U, P]), ALU.is_equal).then_inc(s_hot, 1)

                def scores(n, r):
                    dve.wait_ge(s_dist, n + 3)
                    c = n * 4
                    nc.vector.tensor_reduce(edge_v, d8[r % 2], AX.X, ALU.add).then_inc(s_c3, 1)
                    dve.wait_ge(s_c3, c + 1)
                    nc.vector.tensor_tensor(sc3[:, 0], kept[:, bass.ds(n * U, U), HE:GW], edge_v[:, :, 0:NH], ALU.add).then_inc(s_c3, 1)
                    dve.wait_ge(s_c3, c + 2)
                    nc.vector.scalar_tensor_tensor(sc3[:, 1], sc3[:, 0], 0.2, sc3[:, 0], ALU.mult, ALU.max).then_inc(s_c3, 1)
                    dve.wait_ge(s_c3, c + 3)
                    nc.vector.tensor_tensor(sc3[:, 0], sc3[:, 1], edge_v[:, :, NH:2 * NH], ALU.subtract).then_inc(s_c3, 1)
                    dve.wait_ge(s_c3, c + 4)
                    nc.vector.tensor_scalar(sc3[:, 2], sc3[:, 0], 0.0, None, ALU.min).then_inc(s_sc, 1)

                def messages(n, r):
                    dve.wait_ge(s_ex, n + 1)
                    nc.vector.tensor_tensor(
                        msg[:, r % 2, :, 0:HE].rearrange("p u (j e) -> p u j e", j=NH),
                        kept[:, bass.ds(n * U, U), 0:HE].rearrange("p u (j e) -> p u j e", j=NH),
                        msg[:, r % 2, :, HE:GW].unsqueeze(3).broadcast_to([P, U, NH, NE]), ALU.mult).then_inc(s_msg, 1)

                def adds(n, r):
                    dve.wait_ge(s_mm, n + 3)
                    for k in range(U):
                        if k % 8 == 0:
                            block_at = load_blocks(mybir.EngineType.DVE, 1, n * U + k)
                        to = AGG[:, bass.ds(block_at[k % 8], 1)].rearrange("p a k -> p (a k)")
                        nc.vector.tensor_tensor(to, to, ps[:, 6 + r % 2, k * GW:(k + 1) * GW], ALU.add).then_inc(s_loc, 1)
                        dve.wait_ge(s_loc, k + 1)
                    dve.sem_clear(s_loc)
                    dve.sem_inc(s_add, 1)
                skewed(dve, halves, (0, hots), (2, scores), (2, messages), (3, adds), period=6)

            @block.tensor
            def _(pe):
                pe.sem_inc(s_mm, 2)
                pe.sem_inc(s_mm3, 3)
                pe.sem_inc(s_dist, 2)

                def turn(n, r):
                    pe.wait_ge(s_hot, n + 1)
                    pe.wait_ge(s_tc, n + 1)
                    for k in range(U):
                        mm = nc.tensor.transpose(ps[:, k // 4, (k % 4) * P:(k % 4 + 1) * P], hot3[r % 3][:, k], ident[:])
                    mm.then_inc(s_tp, 1)

                def distribute(n, r):
                    pe.wait_ge(s_tc, n + 2)
                    pe.wait_ge(s_vst, n + 1)
                    for k in range(U):
                        mm = nc.tensor.matmul(ps[:, 4 + r % 2, k * 6 * NH:(k + 1) * 6 * NH], oht[:, k],
                                              vst[:, r % 2, k], start=True, stop=True, skip_group_check=True)
                    mm.then_inc(s_dist, 1)

                def products(n, r):
                    pe.wait_ge(s_msg, n + 1)
                    pe.wait_ge(s_add, n + 1)
                    for k in range(U):
                        mm = nc.tensor.matmul(ps[:, 6 + r % 2, k * GW:(k + 1) * GW], hot3[r % 3][:, k], msg[:, r % 2, k],
                                              start=True, stop=True, skip_group_check=True)
                    mm.then_inc(s_mm, 1)
                    pe.wait_ge(s_mm, n + 3)
                    pe.sem_inc(s_mm3, 1)
                skewed(pe, halves, (1, distribute), (0, turn), (2, products), period=6)

            @block.scalar
            def _(act):
                act.sem_inc(s_tc, 1)

                def turned(n, r):
                    act.wait_ge(s_tp, n + 1)
                    act.wait_ge(s_dist, n + 2)
                    nc.scalar.copy(oht.rearrange("p u m -> p (u m)"), ps[:, 0:4].rearrange("p a f -> p (a f)")).then_inc(s_tc, 1)

                def weights(n, r):
                    act.wait_ge(s_sc, n + 1)
                    act.wait_ge(s_mm, n + 1)
                    nc.scalar.activation(msg[:, r % 2, :, HE:GW], sc3[:, 2], ACT.Exp).then_inc(s_ex, 1)
                skewed(act, halves, (2, weights), (0, turned), period=6)

            @block.gpsimd
            def _(pool):
                with pool.Fori(0, G2) as g:
                    for r in range(2):
                        hold(pool, s_dist, g * 2 + (r + 1))
                        for k in range(U):
                            if k % 8 == 0:
                                block_at = load_blocks(mybir.EngineType.Pool, 1, g * (2 * U) + (r * U + k))
                            ins = nc.gpsimd.tensor_copy(vst[:, r, k], V3[:, bass.ds(block_at[k % 8], 1)].rearrange("p a f c -> p (a f c)"))
                        ins.then_inc(s_vst, 1)

        end_phase()

        s_r, s_rs, s_re, s_rv = sem("route_chain"), sem("route_std"), sem("route_exp"), sem("route_var")
        a16 = small[:, 0]
        t16 = small[:, 1]
        u16 = small[:, 2]
        with nc.Block() as block:
            @block.vector
            def _(dve):
                link = Chain(dve, s_r)
                link(nc.vector.tensor_scalar(emx[:], AGG[:, :, HE:GW], 1e-16, None, ALU.add))
                link(nc.vector.reciprocal(emx[:], emx[:]))
                for j in range(NH):
                    link(nc.vector.tensor_tensor(a16[:, :, j * NE:(j + 1) * NE], AGG[:, :, j * NE:(j + 1) * NE],
                                                 emx[:, :, j:j + 1].broadcast_to([P, NB, NE]), ALU.mult))
                row = lambda i: row16[:, i].unsqueeze(1).broadcast_to([P, NB, HE])
                link(nc.vector.tensor_tensor(t16, a16, row(2), ALU.add))
                m = mv[:, :, 0:1]
                link(nc.vector.tensor_reduce(mv[:, :, 0], t16, AX.X, ALU.add))
                link(nc.vector.tensor_scalar(mv[:, :, 1], mv[:, :, 0], 1.0 / HE, None, ALU.mult))
                link(nc.vector.tensor_tensor(a16, t16, mv[:, :, 1:2].broadcast_to([P, NB, HE]), ALU.subtract))
                link(nc.vector.tensor_tensor(t16, a16, a16, ALU.mult))
                link(nc.vector.tensor_reduce(mv[:, :, 0], t16, AX.X, ALU.add))
                dve.sem_inc(s_rv, 1)
                dve.wait_ge(s_rs, 1)
                link(nc.vector.reciprocal(rstd[:], rstd[:]))
                link(nc.vector.tensor_tensor(t16, a16, rstd[:].unsqueeze(2).broadcast_to([P, NB, HE]), ALU.mult))
                link(nc.vector.tensor_tensor(a16, t16, row(3), ALU.mult))
                link(nc.vector.tensor_tensor(t16, a16, row(4), ALU.add))
                link(nc.vector.tensor_reduce(gates[:], t16.rearrange("p b (h e) -> p b e h", e=NE), AX.X, ALU.add))
                link(nc.vector.tensor_scalar(gates[:], gates[:], 1.0 / NH, None, ALU.mult))
                wins = u16[:, :, 0:NE]
                beat = u16[:, :, NE:NE + 1]
                link(nc.vector.memset(u16, 0.0))
                for lo in range(NE):
                    for hi in range(lo + 1, NE):
                        link(nc.vector.tensor_tensor(beat, gates[:, :, lo:lo + 1], gates[:, :, hi:hi + 1], ALU.is_ge))
                        link(nc.vector.tensor_tensor(wins[:, :, lo:lo + 1], wins[:, :, lo:lo + 1], beat, ALU.add))
                        link(nc.vector.tensor_tensor(beat, gates[:, :, lo:lo + 1], gates[:, :, hi:hi + 1], ALU.is_lt))
                        link(nc.vector.tensor_tensor(wins[:, :, hi:hi + 1], wins[:, :, hi:hi + 1], beat, ALU.add))
                link(nc.vector.tensor_reduce(mv[:, :, 1], gates[:], AX.X, ALU.max))
                ex = u16[:, :, 2 * NE:3 * NE]
                link(nc.vector.tensor_tensor(ex, gates[:], mv[:, :, 1:2].broadcast_to([P, NB, NE]), ALU.subtract))
                dve.sem_inc(s_rv, 1)
                dve.wait_ge(s_re, 1)
                link(nc.vector.scalar_tensor_tensor(ex, wins, float(NE - 2), gates[:], ALU.is_ge, ALU.mult))
                link(nc.vector.tensor_reduce(mv[:, :, 0], ex, AX.X, ALU.add))
                link(nc.vector.reciprocal(rstd[:], mv[:, :, 0]))
                link(nc.vector.tensor_tensor(gates[:], ex, rstd[:].unsqueeze(2).broadcast_to([P, NB, NE]), ALU.mult))

            @block.scalar
            def _(act):
                act.wait_ge(s_rv, 1)
                nc.scalar.activation(rstd[:], mv[:, :, 0], ACT.Sqrt, bias=eps[:, 0:1], scale=1.0 / HE).then_inc(s_rs, 1)
                act.wait_ge(s_rv, 2)
                nc.scalar.activation(gates[:], u16[:, :, 2 * NE:3 * NE], ACT.Exp).then_inc(s_re, 1)

        end_phase()

        o = 0

        def part(n):
            nonlocal o
            v = acc[:, o:o + n]
            o += n
            return v
        w1 = part(NE * KD * HID).rearrange("p (e k n) -> p e k n", e=NE, k=KD)
        w2 = part(NE * KH * D).rearrange("p (e k n) -> p e k n", e=NE, k=KH)
        b1 = part(NE * KH).rearrange("p (e k) -> p e k", e=NE)
        b2 = part(NE * D).rearrange("p (e n) -> p e n", e=NE)
        xt = part(2 * 2 * D).rearrange("p (r a k n) -> p r a k n", r=2, a=2, k=KD)
        hid = part(2 * KH * 2 * P).rearrange("p (r k n) -> p r k n", r=2, k=KH)
        ysum = part(2 * 2 * D).rearrange("p (r a f) -> p r a f", r=2, a=2)
        s_ew = sem("expert_weights")
        s_xt = [sem(f"xn_t_in{r}") for r in range(2)]
        s_x1 = [sem(f"x1_in{r}") for r in range(2)]
        s_yb, s_up, s_gl, s_dn, s_yc, s_done, s_out = (sem(c) for c in (
            "bias_added", "up_done", "gelu_done", "down_done", "expert_added", "pair_done", "rows_out"))
        with nc.Block() as block:
            @block.sync
            def _(sp):
                sp.dma_start(w1, ew1.rearrange("e (k p) n -> p e k n", p=P)).then_inc(s_ew, 16)
                sp.dma_start(w2, ew2.rearrange("e (k p) n -> p e k n", p=P)).then_inc(s_ew, 16)
                sp.dma_start(b1, eb1.rearrange("e (k p) -> p e k", p=P), allow_slow_non_contiguous=True).then_inc(s_ew, 16)
                sp.dma_start(b2.rearrange("p e n -> p (e n)"), eb2.rearrange("(a e) n -> a (e n)", a=1).broadcast_to([P, NE * D])).then_inc(s_ew, 16)

                def loads(g, r):
                    sp.dma_start(xt[:, r].rearrange("p a k n -> p a (k n)"),
                                 xnt_dram[bass.ds(g * 2, 2)].rearrange("a p f -> p a f")).then_inc(s_xt[r], 16)
                    sp.dma_start(ysum[:, r], x1_dram[bass.ds(g * 2 * P, 2 * P)].rearrange(
                        "(a p) f -> p a f", p=P)).then_inc(s_x1[r], 16)
                loads(0, 0)
                loads(1, 1)
                def store(g, r, more):
                    hold(sp, s_done, g + 1)
                    sp.dma_start(out[bass.ds(g * 2 * P, 2 * P)].rearrange("(a p) f -> p a f", p=P),
                                 ysum[:, r]).then_inc(s_out, 16)
                    hold(sp, s_out, g * 16 + 16)
                    if more:
                        loads(g + 2, r)
                with sp.Fori(0, (PAIRS - 3) // 2) as q:
                    for r in range(2):
                        store(q * 2 + r, r, True)
                store(PAIRS - 3, 0, True)
                store(PAIRS - 2, 1, False)
                g = PAIRS - 1
                sp.wait_ge(s_done, PAIRS)
                sp.dma_start(out[g * 2 * P:g * 2 * P + P], ysum[:, 0, 0]).then_inc(s_out, 16)
                sp.dma_start(out[g * 2 * P + P:N], ysum[0:TAIL, 0, 1]).then_inc(s_out, 16)
                sp.wait_ge(s_out, 16 * (PAIRS + 1))

            def pairs(eng, body):
                with eng.Fori(0, (PAIRS - 1) // 2) as q:
                    for r in range(2):
                        body(q * 2 + r, r, q + 1)
                body(PAIRS - 1, 0, (PAIRS - 1) // 2 + 1)

            @block.tensor
            def _(pe):
                pe.wait_ge(s_ew, 64)

                def body(g, r, uses):
                    pe.wait_ge(s_xt[r], uses * 16)
                    for e in range(NE):
                        pe.wait_ge(s_gl, g * NE + (e + 1))
                        for m in range(KH):
                            for k in range(KD):
                                mm = nc.tensor.matmul(
                                    ps[:, 2 * (e % 2) + m // 2, (m % 2) * 2 * P:(m % 2 + 1) * 2 * P],
                                    w1[:, e, k, m * P:(m + 1) * P], xt[:, r, :, k],
                                    start=(k == 0), stop=(k == KD - 1), skip_group_check=True)
                        mm.then_inc(s_up, 1)
                        if e > 0:
                            down(g, e - 1)
                    down(g, NE - 1)

                def down(g, e):
                    pe.wait_ge(s_gl, g * NE + (e + 3))
                    pe.wait_ge(s_yc, g * NE + (e + 1))
                    for a in range(2):
                        to = ps[:, 4 + e % 2, a * D:(a + 1) * D]
                        for m in range(KH):
                            mm = nc.tensor.matmul(to, hid[:, e % 2, m, a * P:(a + 1) * P], w2[:, e, m],
                                                  start=(m == 0), stop=(m == KH - 1), skip_group_check=True)
                    mm.then_inc(s_dn, 1)
                pairs(pe, body)

            @block.scalar
            def _(act):
                act.sem_inc(s_gl, 2)

                def body(g, r, uses):
                    for e in range(NE):
                        act.wait_ge(s_up, g * NE + (e + 1))
                        act.wait_ge(s_dn, g * NE + (e + 1))
                        for m in range(KH):
                            ge = nc.scalar.activation(hid[:, e % 2, m], ps[:, 2 * (e % 2) + m // 2, (m % 2) * 2 * P:(m % 2 + 1) * 2 * P],
                                                      ACT.Gelu, bias=b1[:, e, m:m + 1])
                        ge.then_inc(s_gl, 1)
                pairs(act, body)

            @block.vector
            def _(dve):
                dve.wait_ge(s_ew, 64)
                dve.sem_inc(s_yc, 2)
                dve.sem_inc(s_dn, 2)

                def body(g, r, uses):
                    dve.wait_ge(s_x1[r], uses * 16)
                    for e in range(NE):
                        for a in range(2):
                            add = nc.vector.scalar_tensor_tensor(
                                ysum[:, r, a], b2[:, e], gates[:, bass.ds(g * 2 + a, 1), e], ysum[:, r, a],
                                ALU.mult, ALU.add)
                        add.then_inc(s_yb, 1)
                        dve.wait_ge(s_yb, g * NE + (e + 1))
                        dve.wait_ge(s_dn, g * NE + (e + 3))
                        for a in range(2):
                            add = nc.vector.scalar_tensor_tensor(
                                ysum[:, r, a], ps[:, 4 + e % 2, a * D:(a + 1) * D],
                                gates[:, bass.ds(g * 2 + a, 1), e], ysum[:, r, a], ALU.mult, ALU.add)
                        add.then_inc(s_yc, 1)
                        dve.wait_ge(s_yc, g * NE + (e + 3))
                    dve.sem_inc(s_done, 1)
                pairs(dve, body)


INS = ["x", "src", "dst", "L0_gnn_W1", "L0_gnn_b1", "L0_gnn_W2", "L0_gnn_b2", "L0_gnn_W3", "L0_gnn_b3",
       "L0_ffn_W_gat", "L0_ffn_att_src", "L0_ffn_att_dst", "L0_ffn_b_gat", "L0_ffn_ln_gamma", "L0_ffn_ln_beta",
       "L0_ffn_W1", "L0_ffn_b1", "L0_ffn_W2", "L0_ffn_b2", "L0_ffn_edge_index"]


def kernel(**inputs):
    import numpy as np
    import concourse.bacc as bacc
    from concourse.bass_utils import run_bass_kernel_spmd

    nc = bacc.Bacc("TRN2", target_bir_lowering=False, num_devices=1)
    arrays, a = {}, {}
    for name in INS:
        v = np.ascontiguousarray(inputs[name])
        arrays[name + "_in"] = v
        a[name] = nc.dram_tensor(name + "_in", v.shape, mybir.dt.from_np(v.dtype), kind="ExternalInput").ap()
    out = nc.dram_tensor("out", inputs["x"].shape, F32, kind="ExternalOutput").ap()
    build(nc, a["x"], a["src"], a["dst"], [a[f"L0_gnn_W{i}"] for i in (1, 2, 3)], [a[f"L0_gnn_b{i}"] for i in (1, 2, 3)],
          a["L0_ffn_W_gat"], a["L0_ffn_att_src"], a["L0_ffn_att_dst"], a["L0_ffn_b_gat"], a["L0_ffn_ln_gamma"],
          a["L0_ffn_ln_beta"], a["L0_ffn_W1"], a["L0_ffn_b1"], a["L0_ffn_W2"], a["L0_ffn_b2"],
          a["L0_ffn_edge_index"], out)
    r = run_bass_kernel_spmd(nc, [arrays], core_ids=[0])
    return r.results[0]["out"]
```
